# Optimizing a Trainium2 kernel written in Bass

```python
import numpy as np
import jax
import jax.numpy as jnp

def _softmax(x, axis=-1):
    return jax.nn.softmax(x, axis=axis)

def _gelu(x):
    return jax.nn.gelu(x, approximate=True)

def _silu(x):
    return jax.nn.silu(x)

def _sigmoid(x):
    return jax.nn.sigmoid(x)

def _layernorm(x, axis=-1, eps=1e-05):
    m = jnp.mean(x, axis=axis, keepdims=True)
    v = jnp.var(x, axis=axis, keepdims=True)
    return (x - m) / jnp.sqrt(v + eps)

def _scatter_add(tgt, idx, src, axis=0):
    return tgt.at[idx].add(src)

def _segment_sum(src, seg, n):
    return jax.ops.segment_sum(src, seg, n)
kernel_name = 'mk_prb_d1_jaxref_r4_5a2ba7'

def setup_inputs(seed: int=0):
    np.random.seed(seed)
    _w = jnp.asarray

    def _L0_attn_setup():
        import jax, jax.numpy as jnp
        import numpy as np
        DIM = 512
        N_HEADS = 16
        KV_RANK = 128
        NOPE = 128
        ROPE = 64
        VDIM = 128
        QK_HEAD = NOPE + ROPE
        THETA = 10000.0
        EPS = 1e-06
        SCALE = QK_HEAD ** (-0.5)
        NEG_INF = -1e+30

        def precompute_freqs(seq_len, head_dim, theta=THETA):
            freqs = 1.0 / theta ** (np.arange(0, head_dim, 2, dtype=np.float32) / head_dim)
            ang = np.outer(np.arange(seq_len, dtype=np.float32), freqs)
            return (jnp.asarray(np.cos(ang)), jnp.asarray(np.sin(ang)))

        def apply_rope(x, cos, sin):
            x2 = x.reshape(*x.shape[:-1], -1, 2)
            x0, x1 = (x2[..., 0], x2[..., 1])
            c = cos[None, :, None, :]
            s = sin[None, :, None, :]
            r0 = x0 * c - x1 * s
            r1 = x0 * s + x1 * c
            return jnp.stack([r0, r1], axis=-1).reshape(x.shape)

        def rmsnorm(x, w, eps=EPS):
            rms = jnp.sqrt(jnp.mean(x * x, axis=-1, keepdims=True) + eps)
            return x / rms * w
        key = jax.random.key(seed)
        ks = jax.random.split(key, 5)
        B, S = (2, 512)
        sc = lambda n: 1.0 / np.sqrt(n)
        return {'x': jax.random.normal(ks[0], (B, S, DIM), jnp.float32), 'wq': jax.random.normal(ks[1], (N_HEADS * QK_HEAD, DIM), jnp.float32) * sc(DIM), 'wkv_a': jax.random.normal(ks[2], (KV_RANK + ROPE, DIM), jnp.float32) * sc(DIM), 'wkv_b': jax.random.normal(ks[3], (N_HEADS * (NOPE + VDIM), KV_RANK), jnp.float32) * sc(KV_RANK), 'wo': jax.random.normal(ks[4], (DIM, N_HEADS * VDIM), jnp.float32) * sc(N_HEADS * VDIM), 'kv_norm_w': jnp.ones((KV_RANK,), jnp.float32)}
    _L0_attn_in = _L0_attn_setup()

    def _L0_ffn_setup():
        import jax, jax.numpy as jnp
        import numpy as np
        B, S, D_IN, D_OUT = (4, 512, 512, 512)
        EPS = 1e-10
        key = jax.random.key(seed)
        kx, kw, kb = jax.random.split(key, 3)
        x = jax.random.normal(kx, (B, S, D_IN), dtype=jnp.float32)
        weight = jax.random.normal(kw, (D_OUT, D_IN), dtype=jnp.float32) * 0.02
        bias = jax.random.normal(kb, (D_OUT,), dtype=jnp.float32) * 0.02
        return {'x': x, 'weight': weight, 'bias': bias}
    _L0_ffn_in = _L0_ffn_setup()
    _d = {'L0_attn_x': _L0_attn_in['x'], 'L0_attn_wq': _L0_attn_in['wq'], 'L0_attn_wkv_a': _L0_attn_in['wkv_a'], 'L0_attn_wkv_b': _L0_attn_in['wkv_b'], 'L0_attn_wo': _L0_attn_in['wo'], 'L0_attn_kv_norm_w': _L0_attn_in['kv_norm_w'], 'L0_ffn_weight': _L0_ffn_in['weight'], 'L0_ffn_bias': _L0_ffn_in['bias']}
    _x0 = _d['L0_attn_x']
    _d['L0_attn_x'] = jax.random.normal(jax.random.fold_in(jax.random.key(seed), 1), (1, 2048, 512), dtype=_x0.dtype)
    del _x0
    return _d

def reference(L0_attn_x, L0_attn_wq, L0_attn_wkv_a, L0_attn_wkv_b, L0_attn_wo, L0_attn_kv_norm_w, L0_ffn_weight, L0_ffn_bias):

    def _L0_attn_ref(x, wq, wkv_a, wkv_b, wo, kv_norm_w):
        import jax, jax.numpy as jnp
        import numpy as np
        DIM = 512
        N_HEADS = 16
        KV_RANK = 128
        NOPE = 128
        ROPE = 64
        VDIM = 128
        QK_HEAD = NOPE + ROPE
        THETA = 10000.0
        EPS = 1e-06
        SCALE = QK_HEAD ** (-0.5)
        NEG_INF = -1e+30

        def precompute_freqs(seq_len, head_dim, theta=THETA):
            freqs = 1.0 / theta ** (np.arange(0, head_dim, 2, dtype=np.float32) / head_dim)
            ang = np.outer(np.arange(seq_len, dtype=np.float32), freqs)
            return (jnp.asarray(np.cos(ang)), jnp.asarray(np.sin(ang)))

        def apply_rope(x, cos, sin):
            x2 = x.reshape(*x.shape[:-1], -1, 2)
            x0, x1 = (x2[..., 0], x2[..., 1])
            c = cos[None, :, None, :]
            s = sin[None, :, None, :]
            r0 = x0 * c - x1 * s
            r1 = x0 * s + x1 * c
            return jnp.stack([r0, r1], axis=-1).reshape(x.shape)

        def rmsnorm(x, w, eps=EPS):
            rms = jnp.sqrt(jnp.mean(x * x, axis=-1, keepdims=True) + eps)
            return x / rms * w
        B, S, _ = x.shape
        cos, sin = precompute_freqs(S, ROPE)
        q = (x @ wq.T).reshape(B, S, N_HEADS, QK_HEAD)
        q_nope, q_pe = (q[..., :NOPE], q[..., NOPE:])
        q_pe = apply_rope(q_pe, cos, sin)
        kv = x @ wkv_a.T
        kv_lat, k_pe = (kv[..., :KV_RANK], kv[..., KV_RANK:])
        k_pe = apply_rope(k_pe[:, :, None, :], cos, sin)[:, :, 0, :]
        wkv_b_h = wkv_b.reshape(N_HEADS, NOPE + VDIM, KV_RANK)
        q_lat = jnp.einsum('bshd,hdc->bshc', q_nope, wkv_b_h[:, :NOPE])
        kv_cache = rmsnorm(kv_lat, kv_norm_w)
        scores = (jnp.einsum('bshc,btc->bsht', q_lat, kv_cache) + jnp.einsum('bshr,btr->bsht', q_pe, k_pe)) * SCALE
        causal = jnp.tril(jnp.ones((S, S), bool))
        scores = jnp.where(causal[None, :, None, :], scores, NEG_INF)
        attn = jax.nn.softmax(scores, axis=-1)
        out_lat = jnp.einsum('bsht,btc->bshc', attn, kv_cache)
        out = jnp.einsum('bshc,hdc->bshd', out_lat, wkv_b_h[:, NOPE:])
        return out.reshape(B, S, N_HEADS * VDIM) @ wo.T

    def _L0_ffn_ref(x, weight, bias):
        import jax, jax.numpy as jnp
        import numpy as np
        B, S, D_IN, D_OUT = (4, 512, 512, 512)
        EPS = 1e-10
        scale = jnp.mean(jnp.abs(weight))
        w_t = jnp.clip(jnp.round(weight / (scale + EPS)), -1.0, 1.0)
        w_ste = weight + jax.lax.stop_gradient(w_t * scale - weight)
        return jnp.einsum('bsi,oi->bso', x, w_ste) + bias
    x = L0_attn_x
    xn = _layernorm(x, axis=-1)
    x = x + _L0_attn_ref(xn, L0_attn_wq, L0_attn_wkv_a, L0_attn_wkv_b, L0_attn_wo, L0_attn_kv_norm_w) + _L0_ffn_ref(xn, L0_ffn_weight, L0_ffn_bias)
    return x

_drawn_inputs = setup_inputs


def setup_inputs(seed=0):
    import zlib

    import numpy as np

    out = dict(_drawn_inputs(seed))
    spreads = {'L0_attn_kv_norm_w': (1.0, 0.2)}
    factors = {'L0_ffn_bias': 3.017}
    for name, (base, spread) in spreads.items():
        noise = np.random.default_rng([zlib.crc32(name.encode()), seed]).standard_normal(out[name].shape)
        drawn = base * np.exp(spread * noise) if base else spread * noise
        out[name] = jnp.asarray(drawn.astype(out[name].dtype))
    for name, factor in factors.items():
        out[name] = (out[name] * factor).astype(out[name].dtype)
    return out
```

```python
from contextlib import ExitStack

import numpy as np

import concourse.bass as bass
from concourse import mybir

ALU = mybir.AluOpType
ACT = mybir.ActivationFunctionType
AXX = mybir.AxisListType.X
F32 = mybir.dt.float32
F32R = mybir.dt.float32r
BF16 = mybir.dt.bfloat16
ENG = mybir.EngineType

P = 128
S = 2048
D = 512
H = 16
NOPE = 128
ROPE = 64
HALF = ROPE // 2
RANK = 128
VDIM = 128
QK = NOPE + ROPE
IT = D // P
CW = 512
NCH = S // CW
QB = CW // P
NT = S // P
SCALE = float(QK) ** -0.5
MASKED = -1.0e30
LN_EPS = 1e-5
RMS_EPS = 1e-6
FFN_EPS = 1e-10
LOWEST = -3.0e38
PT_RING = 3


def need(eng, sem, value):
    if isinstance(value, int) and value <= 0:
        return
    eng.wait_ge(sem, value)


def heads_before(pos):
    j, m, p = pos
    return H * j + 2 * m + p


def tiles_before(pos):
    j, m, p = pos
    return QB * H * (j * (j + 1) // 2) + QB * (j + 1) * (2 * m + p)


def rows_before(pos):
    return QB * heads_before(pos)


def same_parity_before(pos):
    j, m, p = pos
    return (H // 2) * j + m


def tiles_of(pos):
    return QB * (pos[0] + 1)


def first_of_chunk(pos):
    return isinstance(pos[1], int) and pos[1:] == (0, 0)


def first_row(pos, k):
    return max(0, k - QB * pos[0])


def walk(nc, engine, step):
    def two_steps(j, m):
        step((j, m, 1), (j, m, 0), (j, m + 1, 0))
        step((j, m + 1, 0), (j, m, 1), (j, m + 1, 1))

    for j in range(NCH):
        step((j, 0, 0), (j - 1, H // 2 - 1, 1) if j else None, (j, 0, 1))
        if j == 0:
            two_steps(0, 0)
        with nc.Fori(0 if j else 1, H // 2 - 1, engines=[engine]) as m:
            two_steps(j, m)
        step((j, H // 2 - 1, 1), (j, H // 2 - 1, 0), (j + 1, 0, 0) if j + 1 < NCH else None)
    step(None, (NCH - 1, H // 2 - 1, 1), None)


def build_tokens(nc, t, keep):
    with ExitStack() as ctx:
        def sb(name, shape, dt=F32):
            return ctx.enter_context(nc.sbuf_tensor(name, shape, dt))

        def ps(name, shape):
            return ctx.enter_context(nc.psum_tensor(name, shape, F32))

        def sem(name):
            return ctx.enter_context(nc.semaphore(name))

        w_ffn = sb("w_ffn", [P, IT, D])
        w_pos = sb("w_pos", [P, IT * D])
        w_neg = sb("w_neg", [P, IT * D])
        w_tern = sb("w_tern", [P, IT * D])
        w_ste = sb("w_ste", [P, IT, D])
        ffnT_h = sb("ffnT_h", [P, IT, D], F32R)
        ffnT_l = sb("ffnT_l", [P, IT, D], F32R)
        w_kva = sb("w_kva", [96, 2, D])
        kvaT_h = sb("kvaT_h", [P, IT, 192], F32R)
        kvaT_l = sb("kvaT_l", [P, IT, 192], F32R)
        rows = sb("rows", [1, D + RANK])
        ones = sb("ones", [P, P])
        bias_all = sb("bias_all", [P, D])
        norm_all = sb("norm_all", [P, RANK])
        wsum = sb("wsum", [P, 8])
        minus_half = sb("minus_half", [P, QB])
        x_in = sb("x_in", [P, QB, D])
        xhat = sb("xhat", [P, QB, D])
        xb = sb("xb", [P, QB, D])
        stats = sb("stats", [P, QB, 6])
        moments = sb("moments", [P, QB, 2])
        var_eps = sb("var_eps", [P, QB])
        rstd = sb("rstd", [P, QB])
        xT_h = sb("xT_h", [P, IT, CW], F32R)
        xT_l = sb("xT_l", [P, IT, CW], F32R)
        acc0 = sb("acc0", [P, QB, D])
        squares = sb("squares", [P, RANK])
        sumsq = sb("sumsq", [P, QB])
        ms = sb("ms", [P, QB])
        rrms = sb("rrms", [P, QB])
        lat = sb("lat", [P, QB, RANK])
        by_cos = sb("by_cos", [P, QB, ROPE])
        by_sin = sb("by_sin", [P, QB, ROPE])
        roped = sb("roped", [P, QB, ROPE])
        kpe = sb("kpe", [P, QB, 2, 2, HALF], F32R)
        cosN = sb("cosN", [P, NT, ROPE])
        sinN = sb("sinN", [P, NT, ROPE])

        pX = [ps(f"pX{i}", [P, IT, P]) for i in range(2)]
        pKV = [ps(f"pKV{i}", [P, 512]) for i in range(2)]
        pF = [ps(f"pF{i}", [P, D]) for i in range(2)]
        pK = [ps(f"pK{i}", [P, 4, P]) for i in range(2)]
        ident = keep["ident"]

        s_const = sem("s_const")
        s_w = sem("s_w")
        s_ones = sem("s_ones")
        s_bcast = sem("s_bcast")
        s_bcast_out = sem("s_bcast_out")
        s_abs = sem("s_abs")
        s_total = sem("s_total")
        s_thr = sem("s_thr")
        s_tern = sem("s_tern")
        s_wT = sem("s_wT")
        s_wT_h = sem("s_wT_h")
        s_wT_l = sem("s_wT_l")
        s_aT = sem("s_aT")
        s_aT_h = sem("s_aT_h")
        s_aT_l = sem("s_aT_l")
        s_x = sem("s_x")
        s_stats = sem("s_stats")
        s_moments = sem("s_moments")
        s_var = sem("s_var")
        s_rstd = sem("s_rstd")
        s_xhat = sem("s_xhat")
        s_xb = sem("s_xb")
        s_xT = sem("s_xT")
        s_xT_h = sem("s_xT_h")
        s_xT_l = sem("s_xT_l")
        s_kv = sem("s_kv")
        s_sumsq = sem("s_sumsq")
        s_ms = sem("s_ms")
        s_rrms = sem("s_rrms")
        s_rot = sem("s_rot")
        s_lat = sem("s_lat")
        s_roped = sem("s_roped")
        s_vh = sem("s_vh")
        s_kpe_h = sem("s_kpe_h")
        s_kpe_l = sem("s_kpe_l")
        s_ffn = sem("s_ffn")
        s_acc = sem("s_acc")
        s_kT = sem("s_kT")
        s_kT_h = sem("s_kT_h")
        s_kT_l = sem("s_kT_l")
        s_stored = sem("s_stored")

        block = ctx.enter_context(nc.Block())

        @block.sync
        def _(sp):
            sp.dma_start(ident[:, :], t["ident"]).then_inc(s_const, 16)
            sp.dma_start(w_kva[:, :, :], t["wkv_a"].rearrange("(a p) i -> p a i", p=96)).then_inc(s_w, 16)
            sp.dma_start(w_ffn[:, :, :], t["w_ffn"].rearrange("(a p) i -> p a i", p=P)).then_inc(s_w, 16)
            sp.dma_start(rows[:, 0:D], t["b_ffn"].rearrange("(a n) -> a n", a=1)).then_inc(s_const, 16)
            sp.dma_start(rows[:, D:], t["kv_norm_w"].rearrange("(a n) -> a n", a=1)).then_inc(s_const, 16)
            sp.dma_start(cosN[:, :, :], t["cosN"]).then_inc(s_const, 16)
            sp.dma_start(sinN[:, :, :], t["sinN"]).then_inc(s_const, 16)
            sp.dma_start(keep["mask_f32"][:, :], t["mask"]).then_inc(s_const, 16)
            sp.dma_start(keep["dup_f32"][:, :], t["dup"]).then_inc(s_const, 16)
            xc = t["x"].rearrange("(c a p) i -> c p a i", a=QB, p=P)

            def load(c):
                need(sp, s_xhat, QB * c)
                need(sp, s_xb, QB * c)
                sp.dma_start(x_in[:, :, :], xc[c]).then_inc(s_x, 16)

            def store(c):
                need(sp, s_xT_h, QB * (c + 1))
                need(sp, s_xT_l, QB * (c + 1))
                sp.dma_start(t["xT_scr"][c, 0], xT_h[:, :, :].bitcast(F32)).then_inc(s_stored, 16)
                sp.dma_start(t["xT_scr"][c, 1], xT_l[:, :, :].bitcast(F32)).then_inc(s_stored, 16)
                need(sp, s_acc, QB * (c + 1))
                sp.dma_start(t["acc_scr"][c], acc0[:, :, :]).then_inc(s_stored, 16)

            sp.dma_start(x_in[:, :, :], xc[0]).then_inc(s_x, 16)
            load(1)
            store(0)
            with nc.Fori(1, NCH - 1, engines=[ENG.SP]) as c:
                load(c + 1)
                store(c)
            store(NCH - 1)
            need(sp, s_stored, 48 * NCH)

        @block.gpsimd
        def _(pool):
            pool.memset(minus_half[:, :], -0.5).then_inc(s_ones, 1)
            need(pool, s_ones, 2)
            need(pool, s_bcast_out, 2)
            def chunk(c):
                need(pool, s_var, c + 1)
                pool.tensor_tensor(rstd[:, :], var_eps[:, :], minus_half[:, :], ALU.pow).then_inc(s_rstd, 1)
                need(pool, s_acc, QB * c)
                for b in range(QB):
                    need(pool, s_x, 16 * (c + 1))
                    pool.tensor_tensor(xb[:, b, :], x_in[:, b, :], bias_all[:, :], ALU.add).then_inc(s_xb, 1)
                for b in range(QB):
                    n = QB * c + b
                    need(pool, s_ms, n + 1)
                    pool.tensor_tensor(rrms[:, b:b + 1], ms[:, b:b + 1], minus_half[:, b:b + 1],
                                       ALU.pow).then_inc(s_rrms, 1)
                    need(pool, s_rot, 2 * n + 2)
                    need(pool, s_kpe_h, QB * c)
                    pool.tensor_tensor(roped[:, b, 0:HALF], by_cos[:, b, 0:HALF], by_sin[:, b, HALF:],
                                       ALU.subtract).then_inc(s_roped, 1)
                    pool.tensor_tensor(roped[:, b, HALF:], by_cos[:, b, HALF:], by_sin[:, b, 0:HALF],
                                       ALU.add).then_inc(s_roped, 1)
                    need(pool, s_kpe_h, n + 1)
                    pool.tensor_tensor(kpe[:, b, :, 1, :], roped[:, b, :].rearrange("p (x f) -> p x f", x=2),
                                       kpe[:, b, :, 0, :].bitcast(F32), ALU.subtract).then_inc(s_kpe_l, 1)
                    need(pool, s_vh, n + 1)
                    pool.tensor_tensor(keep["V_l"][:, bass.ds(n, 1), :].rearrange("p a c -> p (a c)"), lat[:, b, :],
                                       keep["V_h"][:, bass.ds(n, 1), :].rearrange("p a c -> p (a c)").bitcast(F32),
                                       ALU.subtract)

            chunk(0)
            with nc.Fori(1, NCH, engines=[ENG.Pool]) as c:
                chunk(c)

        @block.scalar
        def _(act):
            for it in range(IT):
                need(act, s_wT, it + 1)
                act.activation(ffnT_h[:, it, :], pF[it % 2][:, :], ACT.Copy).then_inc(s_wT_h, 1)
            for a in range(2):
                need(act, s_aT, a + 1)
                src = pX[a][:, :, 0:96]
                if a == 0:
                    act.activation(kvaT_h[:, :, 0:96], src, ACT.Copy).then_inc(s_aT_h, 1)
                else:
                    act.activation(kvaT_h[:, :, 96:128], src[:, :, 0:32], ACT.Copy).then_inc(s_aT_h, 1)
                    for x in range(2):
                        act.activation(kvaT_h[:, :, 128 + HALF * x:128 + HALF * (x + 1)],
                                       src[:, :, 32 + x:96:2], ACT.Copy).then_inc(s_aT_h, 1)
            def chunk(c):
                need(act, s_stored, 48 * c)
                for b in range(QB):
                    need(act, s_xT, QB * c + b + 1)
                    act.activation(xT_h[:, :, b * P:(b + 1) * P], pX[b % 2][:, :, :], ACT.Copy).then_inc(s_xT_h, 1)

                def keys(b):
                    n = QB * c + b
                    need(act, s_kv, n + 1)
                    need(act, s_sumsq, n)
                    act.activation(squares[:, :], pKV[b % 2][:, 0:RANK], ACT.Square,
                                   accum_out=sumsq[:, b:b + 1]).then_inc(s_sumsq, 1)

                def halves(b):
                    n = QB * c + b
                    need(act, s_roped, 2 * n + 2)
                    need(act, s_kT, QB * c)
                    act.activation(kpe[:, b, :, 0, :], roped[:, b, :].rearrange("p (x f) -> p x f", x=2),
                                   ACT.Copy).then_inc(s_kpe_h, 1)
                    need(act, s_lat, n + 1)
                    act.activation(keep["V_h"][:, bass.ds(n, 1), :].rearrange("p a c -> p (a c)"), lat[:, b, :],
                                   ACT.Copy).then_inc(s_vh, 1)

                keys(0)
                for b in range(QB):
                    if b + 1 < QB:
                        keys(b + 1)
                    halves(b)
                for b in range(QB):
                    n = QB * c + b
                    need(act, s_kT, n + 1)
                    act.activation(keep["Kn_h"][:, bass.ds(P * n, P)], pK[b % 2][:, 0, :],
                                   ACT.Copy).then_inc(s_kT_h, 1)
                    act.activation(keep["Kp"][:, bass.ds(P * n, P)], pK[b % 2][:, 1, :],
                                   ACT.Copy).then_inc(s_kT_h, 1)

            chunk(0)
            with nc.Fori(1, NCH, engines=[ENG.Activation]) as c:
                chunk(c)

        @block.vector
        def _(dve):
            dve.memset(ones[:, :], 1.0).then_inc(s_ones, 1)
            need(dve, s_w, 32)
            dve.tensor_reduce(wsum[:, 0:1], w_ffn[:, :, :].rearrange("p a i -> p (a i)"), AXX, ALU.add,
                              apply_absolute_value=True).then_inc(s_abs, 1)
            need(dve, s_total, 1)
            dve.tensor_scalar(wsum[:, 1:2], pK[0][:, 0, 0:1], 1.0 / (D * D), None, ALU.mult).then_inc(s_thr, 1)
            need(dve, s_thr, 1)
            dve.tensor_scalar(wsum[:, 2:3], wsum[:, 1:2], FFN_EPS, 0.5, ALU.add, ALU.mult).then_inc(s_thr, 1)
            dve.tensor_scalar(wsum[:, 4:5], wsum[:, 1:2], FFN_EPS, -0.5, ALU.add, ALU.mult).then_inc(s_thr, 1)
            need(dve, s_thr, 3)
            w_flat = w_ffn[:, :, :].rearrange("p a i -> p (a i)")
            w_out = w_ste[:, :, :].rearrange("p a i -> p (a i)")
            dve.tensor_scalar(w_pos[:, :], w_flat, wsum[:, 2:3], None, ALU.is_gt).then_inc(s_tern, 1)
            dve.tensor_scalar(w_neg[:, :], w_flat, wsum[:, 4:5], None, ALU.is_lt).then_inc(s_tern, 1)
            need(dve, s_tern, 2)
            dve.tensor_tensor(w_tern[:, :], w_pos[:, :], w_neg[:, :], ALU.subtract).then_inc(s_tern, 1)
            need(dve, s_tern, 3)
            dve.scalar_tensor_tensor(out=w_pos[:, :], in0=w_tern[:, :], scalar=wsum[:, 1:2], in1=w_flat,
                                     op0=ALU.mult, op1=ALU.subtract).then_inc(s_tern, 1)
            need(dve, s_tern, 4)
            dve.tensor_tensor(w_out, w_pos[:, :], w_flat, ALU.add).then_inc(s_tern, 1)
            need(dve, s_bcast, 2)
            dve.tensor_copy(bias_all[:, :], pKV[0][:, :]).then_inc(s_bcast_out, 1)
            dve.tensor_copy(norm_all[:, :], pKV[1][:, 0:RANK]).then_inc(s_bcast_out, 1)
            for it in range(IT):
                need(dve, s_wT_h, it + 1)
                dve.tensor_tensor(ffnT_l[:, it, :], pF[it % 2][:, :], ffnT_h[:, it, :].bitcast(F32),
                                  ALU.subtract).then_inc(s_wT_l, 1)
            need(dve, s_aT_h, 4)
            dve.tensor_tensor(kvaT_l[:, :, 0:96], pX[0][:, :, 0:96], kvaT_h[:, :, 0:96].bitcast(F32),
                              ALU.subtract).then_inc(s_aT_l, 1)
            dve.tensor_tensor(kvaT_l[:, :, 96:128], pX[1][:, :, 0:32], kvaT_h[:, :, 96:128].bitcast(F32),
                              ALU.subtract).then_inc(s_aT_l, 1)
            for x in range(2):
                cols = slice(128 + HALF * x, 128 + HALF * (x + 1))
                dve.tensor_tensor(kvaT_l[:, :, cols], pX[1][:, :, 32 + x:96:2], kvaT_h[:, :, cols].bitcast(F32),
                                  ALU.subtract).then_inc(s_aT_l, 1)
            need(dve, s_const, 16 * 7)
            def chunk(c):
                need(dve, s_x, 16 * (c + 1))
                for b in range(QB):
                    dve.bn_stats(stats[:, b, :], x_in[:, b, :]).then_inc(s_stats, 4)
                need(dve, s_ones, 2)
                need(dve, s_stats, 16 * (c + 1))
                for b in range(QB):
                    dve.bn_aggr(moments[:, b, :], stats[:, b, :]).then_inc(s_moments, 1)
                need(dve, s_moments, QB * (c + 1))
                dve.tensor_scalar(var_eps[:, :], moments[:, :, 1], LN_EPS, None, ALU.add).then_inc(s_var, 1)
                need(dve, s_rstd, c + 1)
                need(dve, s_xT, QB * c)
                for b in range(QB):
                    dve.tensor_scalar(xhat[:, b, :], x_in[:, b, :], moments[:, b, 0:1], rstd[:, b:b + 1],
                                      ALU.subtract, ALU.mult).then_inc(s_xhat, 1)
                for b in range(QB):
                    cols = slice(b * P, (b + 1) * P)
                    need(dve, s_xT_h, QB * c + b + 1)
                    dve.tensor_tensor(xT_l[:, :, cols], pX[b % 2][:, :, :], xT_h[:, :, cols].bitcast(F32),
                                      ALU.subtract).then_inc(s_xT_l, 1)

                def linear(b):
                    need(dve, s_ffn, QB * c + b + 1)
                    need(dve, s_xb, QB * c + b + 1)
                    need(dve, s_stored, 48 * c)
                    dve.tensor_tensor(acc0[:, b, :], pF[b % 2][:, :], xb[:, b, :], ALU.add).then_inc(s_acc, 1)

                for b in range(QB):
                    n = QB * c + b
                    pe_cols = pKV[b % 2][:, RANK:RANK + ROPE]
                    need(dve, s_sumsq, n + 1)
                    need(dve, s_roped, 2 * QB * c)
                    dve.tensor_tensor(by_cos[:, b, :], pe_cols,
                                      cosN[:, bass.ds(n, 1), :].rearrange("p a c -> p (a c)"),
                                      ALU.mult).then_inc(s_rot, 1)
                    dve.tensor_tensor(by_sin[:, b, :], pe_cols,
                                      sinN[:, bass.ds(n, 1), :].rearrange("p a c -> p (a c)"),
                                      ALU.mult).then_inc(s_rot, 1)
                    need(dve, s_rrms, QB * c)
                    dve.tensor_scalar(ms[:, b:b + 1], sumsq[:, b:b + 1], 1.0 / RANK, RMS_EPS,
                                      ALU.mult, ALU.add).then_inc(s_ms, 1)
                    if b >= 1:
                        linear(b - 1)
                    need(dve, s_rrms, n + 1)
                    need(dve, s_kT, QB * c)
                    dve.scalar_tensor_tensor(out=lat[:, b, :], in0=pKV[b % 2][:, 0:RANK], scalar=rrms[:, b:b + 1],
                                             in1=norm_all[:, :], op0=ALU.mult, op1=ALU.mult).then_inc(s_lat, 1)
                linear(QB - 1)
                for b in range(QB):
                    n = QB * c + b
                    need(dve, s_kT_h, 2 * n + 2)
                    dve.tensor_tensor(keep["Kn_l"][:, bass.ds(P * n, P)], pK[b % 2][:, 0, :],
                                      keep["Kn_h"][:, bass.ds(P * n, P)].bitcast(F32),
                                      ALU.subtract).then_inc(s_kT_l, 1)

            chunk(0)
            with nc.Fori(1, NCH, engines=[ENG.DVE]) as c:
                chunk(c)

        @block.tensor
        def _(pe):
            need(pe, s_ones, 2)
            need(pe, s_const, 16 * 7)
            pe.matmul(pKV[0][:, :], ones[0:1, :], rows[:, 0:D], start=True, stop=True).then_inc(s_bcast, 1)
            pe.matmul(pKV[1][:, 0:RANK], ones[0:1, :], rows[:, D:], start=True, stop=True).then_inc(s_bcast, 1)
            need(pe, s_abs, 1)
            pe.matmul(pK[0][:, 0, 0:1], ones[:, :], wsum[:, 0:1], start=True, stop=True).then_inc(s_total, 1)
            need(pe, s_w, 32)
            for a in range(2):
                for it in range(IT):
                    mm = pe.transpose(pX[a][:, it, 0:96], w_kva[:, a, it * P:(it + 1) * P], ident[0:96, 0:96])
                mm.then_inc(s_aT, 1)
            need(pe, s_tern, 5)
            for it in range(IT):
                need(pe, s_wT_l, it - 1)
                for a in range(IT):
                    mm = pe.transpose(pF[it % 2][:, a * P:(a + 1) * P], w_ste[:, a, it * P:(it + 1) * P],
                                      ident[:, :])
                mm.then_inc(s_wT, 1)
            need(pe, s_wT_l, IT)
            need(pe, s_aT_l, 4)
            need(pe, s_bcast_out, 2)
            def chunk(c):
                for b in range(QB):
                    n = QB * c + b
                    need(pe, s_xhat, n + 1)
                    if b >= 2:
                        need(pe, s_xT_l, n - 1)
                    for it in range(IT):
                        mm = pe.transpose(pX[b % 2][:, it, :], xhat[:, b, it * P:(it + 1) * P], ident[:, :])
                    mm.then_inc(s_xT, 1)

                def product(out, b, w_h, w_l, done):
                    cols = slice(b * P, (b + 1) * P)
                    for it in range(IT):
                        for k, (xs, ws) in enumerate(((xT_h, w_h), (xT_h, w_l), (xT_l, w_h))):
                            mm = pe.matmul(out, xs[:, it, cols], ws[:, it, :], start=(it == 0 and k == 0),
                                           stop=(it == IT - 1 and k == 2))
                    mm.then_inc(done, 1)

                def latent(b):
                    need(pe, s_xT_l, QB * c + b + 1)
                    if b >= 2:
                        need(pe, s_lat, QB * c + b - 1)
                    product(pKV[b % 2][:, 0:192], b, kvaT_h, kvaT_l, s_kv)

                def linear(b):
                    if b >= 2:
                        need(pe, s_acc, QB * c + b - 1)
                    product(pF[b % 2][:, :], b, ffnT_h, ffnT_l, s_ffn)

                latent(0)
                latent(1)
                for b in range(2, QB):
                    linear(b - 2)
                    latent(b)
                linear(QB - 2)
                linear(QB - 1)
                for b in range(QB):
                    n = QB * c + b
                    if b >= 2:
                        need(pe, s_kT_l, n - 1)
                    need(pe, s_lat, n + 1)
                    pe.transpose(pK[b % 2][:, 0, :], lat[:, b, :], ident[:, :])
                    need(pe, s_kpe_l, n + 1)
                    pe.transpose(pK[b % 2][:, 1, :], kpe[:, b, :, :, :].rearrange("p x h f -> p (x h f)").bitcast(F32),
                                 ident[:, :]).then_inc(s_kT, 1)

            chunk(0)
            with nc.Fori(1, NCH, engines=[ENG.PE]) as c:
                chunk(c)


def build_weights(nc, t, keep):
    with ExitStack() as ctx:
        def sb(name, shape, dt=F32):
            return ctx.enter_context(nc.sbuf_tensor(name, shape, dt))

        def ps(name, shape):
            return ctx.enter_context(nc.psum_tensor(name, shape, F32))

        def sem(name):
            return ctx.enter_context(nc.semaphore(name))

        wqn = [sb(f"wqn{i}", [P, D]) for i in range(2)]
        wqp = [sb(f"wqp{i}", [ROPE, D]) for i in range(2)]
        wkb = [sb(f"wkb{i}", [P, 2, RANK]) for i in range(2)]
        wo = [sb(f"wo{i}", [P, IT, VDIM]) for i in range(2)]
        wqn_h = [sb(f"wqn_h{i}", [P, D], F32R) for i in range(2)]
        wqn_l = [sb(f"wqn_l{i}", [P, D], F32R) for i in range(2)]
        wqp_h = [sb(f"wqp_h{i}", [ROPE, D], F32R) for i in range(2)]
        wqp_l = [sb(f"wqp_l{i}", [ROPE, D], F32R) for i in range(2)]
        wkb_h = [sb(f"wkb_h{i}", [P, 2, RANK], F32R) for i in range(2)]
        wkb_l = [sb(f"wkb_l{i}", [P, 2, RANK], F32R) for i in range(2)]
        woT_h = [sb(f"woT_h{i}", [P, D], F32R) for i in range(2)]
        woT_l = [sb(f"woT_l{i}", [P, D], F32R) for i in range(2)]
        out_q = [sb(f"out_q{i}", [P, 4, IT, P], F32R) for i in range(2)]
        out_v = [sb(f"out_v{i}", [P, 2, D], F32R) for i in range(2)]
        dup = sb("dup", [ROPE, P], F32R)

        p_wo = ps("p_wo", [P, D])
        p_ph = ps("p_ph", [P, IT, P])
        p_pl = ps("p_pl", [P, IT, P])
        p_q = [ps(f"p_q{i}", [P, IT, P]) for i in range(2)]
        p_v = [ps(f"p_v{i}", [P, D]) for i in range(2)]
        ident = keep["ident"]

        s_load = [sem(f"s_load{i}") for i in range(2)]
        s_dup = sem("s_dup")
        s_high = sem("s_high")
        s_low = sem("s_low")
        s_woT = sem("s_woT")
        s_woT_h = sem("s_woT_h")
        s_woT_l = sem("s_woT_l")
        s_pe = sem("s_pe")
        s_pe_h = sem("s_pe_h")
        s_pe_l = sem("s_pe_l")
        s_q = sem("s_q")
        s_q_h = sem("s_q_h")
        s_q_l = sem("s_q_l")
        s_v = sem("s_v")
        s_v_h = sem("s_v_h")
        s_v_l = sem("s_v_l")
        s_stored = [sem(f"s_wstored{i}") for i in range(2)]

        block = ctx.enter_context(nc.Block())
        wq_heads = t["wq"].rearrange("(h r) i -> h r i", h=H)
        wkb_heads = t["wkv_b"].rearrange("(h two d) c -> h d two c", h=H, two=2)
        wo_heads = t["wo"].rearrange("(a p) (h d) -> h p a d", p=P, h=H)

        @block.sync
        def _(sp):
            def load(h, p):
                sp.dma_start(wqn[p][:, :], wq_heads[h][0:NOPE, :]).then_inc(s_load[p], 16)
                sp.dma_start(wqp[p][:, :], wq_heads[h][NOPE:QK, :]).then_inc(s_load[p], 16)
                sp.dma_start(wkb[p][:, :, :], wkb_heads[h]).then_inc(s_load[p], 16)
                sp.dma_start(wo[p][:, :, :], wo_heads[h]).then_inc(s_load[p], 16)

            def store(h, n, p):
                need(sp, s_pe_h, n + 1)
                need(sp, s_pe_l, n + 1)
                need(sp, s_q_l, n + 1)
                sp.dma_start(t["wq_scr"][h], out_q[p][:, :, :, :].bitcast(F32)).then_inc(s_stored[p], 16)
                need(sp, s_v_l, n + 1)
                sp.dma_start(t["wv_scr"][h], out_v[p][:, :, :].bitcast(F32)).then_inc(s_stored[p], 16)

            load(0, 0)
            load(1, 1)
            with nc.Fori(0, H // 2 - 1, engines=[ENG.SP]) as m:
                for p in range(2):
                    h = 2 * m + p
                    need(sp, s_woT, h + 1)
                    need(sp, s_high, 3 * h + 3)
                    need(sp, s_low, 3 * h + 3)
                    load(h + 2, p)
                    store(h, h, p)
            store(H - 2, H - 2, 0)
            store(H - 1, H - 1, 1)
            for p in range(2):
                need(sp, s_stored[p], 16 * H)

        @block.scalar
        def _(act):
            act.activation(keep["mask"][:, :], keep["mask_f32"][:, :], ACT.Copy)
            act.activation(keep["ident16"][:, :], ident[:, :], ACT.Copy)
            act.activation(dup[:, :], keep["dup_f32"][:, :], ACT.Copy).then_inc(s_dup, 1)
            def pair(m):
                for p in range(2):
                    h = 2 * m + p
                    need(act, s_load[p], 64 * (m + 1))
                    need(act, s_v, h - 1)
                    act.activation(wqp_h[p][:, :], wqp[p][:, :], ACT.Copy).then_inc(s_high, 1)
                    act.activation(wkb_h[p][:, :, :], wkb[p][:, :, :], ACT.Copy).then_inc(s_high, 1)
                    act.activation(wqn_h[p][:, :], wqn[p][:, :], ACT.Copy).then_inc(s_high, 1)
                    need(act, s_woT, h + 1)
                    act.activation(woT_h[p][:, :], p_wo[:, :], ACT.Copy).then_inc(s_woT_h, 1)
                    need(act, s_stored[p], 32 * m)
                    need(act, s_pe, h + 1)
                    act.activation(out_q[p][:, 2, :, :], p_ph[:, :, :], ACT.Copy).then_inc(s_pe_h, 1)
                    need(act, s_q, h + 1)
                    act.activation(out_q[p][:, 0, :, :], p_q[p][:, :, :], ACT.Copy).then_inc(s_q_h, 1)
                    need(act, s_v, h + 1)
                    act.activation(out_v[p][:, 0, :], p_v[p][:, :], ACT.Copy).then_inc(s_v_h, 1)

            pair(0)
            with nc.Fori(1, H // 2, engines=[ENG.Activation]) as m:
                pair(m)

        @block.gpsimd
        def _(pool):
            def pair(m):
                for p in range(2):
                    h = 2 * m + p
                    need(pool, s_high, 3 * h + 2)
                    pool.tensor_tensor(wqp_l[p][:, :], wqp[p][:, :], wqp_h[p][:, :].bitcast(F32),
                                       ALU.subtract).then_inc(s_low, 1)
                    pool.tensor_tensor(wkb_l[p][:, :, :], wkb[p][:, :, :], wkb_h[p][:, :, :].bitcast(F32),
                                       ALU.subtract).then_inc(s_low, 1)
                    need(pool, s_high, 3 * h + 3)
                    pool.tensor_tensor(wqn_l[p][:, :], wqn[p][:, :], wqn_h[p][:, :].bitcast(F32),
                                       ALU.subtract).then_inc(s_low, 1)

            pair(0)
            with nc.Fori(1, H // 2, engines=[ENG.Pool]) as m:
                pair(m)

        @block.vector
        def _(dve):
            def pair(m):
                for p in range(2):
                    h = 2 * m + p
                    need(dve, s_woT_h, h + 1)
                    dve.tensor_tensor(woT_l[p][:, :], p_wo[:, :], woT_h[p][:, :].bitcast(F32),
                                      ALU.subtract).then_inc(s_woT_l, 1)
                    need(dve, s_pe, h + 1)
                    need(dve, s_stored[p], 32 * m)
                    dve.tensor_copy(out_q[p][:, 3, :, :], p_pl[:, :, :]).then_inc(s_pe_l, 1)
                    need(dve, s_q_h, h + 1)
                    dve.tensor_tensor(out_q[p][:, 1, :, :], p_q[p][:, :, :], out_q[p][:, 0, :, :].bitcast(F32),
                                      ALU.subtract).then_inc(s_q_l, 1)
                    need(dve, s_v_h, h + 1)
                    dve.tensor_tensor(out_v[p][:, 1, :], p_v[p][:, :], out_v[p][:, 0, :].bitcast(F32),
                                      ALU.subtract).then_inc(s_v_l, 1)

            pair(0)
            with nc.Fori(1, H // 2, engines=[ENG.DVE]) as m:
                pair(m)

        @block.tensor
        def _(pe):
            need(pe, s_dup, 1)
            def pair(m):
                for p in range(2):
                    h = 2 * m + p
                    need(pe, s_load[p], 64 * (m + 1))
                    need(pe, s_woT_l, h)
                    for a in range(IT):
                        mm = pe.transpose(p_wo[:, a * P:(a + 1) * P], wo[p][:, a, :], ident[:, :])
                    mm.then_inc(s_woT, 1)
                    need(pe, s_high, 3 * h + 1)
                    need(pe, s_low, 3 * h + 1)
                    need(pe, s_pe_h, h)
                    need(pe, s_pe_l, h)
                    for out, w in ((p_ph, wqp_h[p]), (p_pl, wqp_l[p])):
                        for it in range(IT):
                            mm = pe.matmul(out[:, it, :], w[:, it * P:(it + 1) * P], dup[:, :],
                                           start=True, stop=True)
                    mm.then_inc(s_pe, 1)
                    need(pe, s_low, 3 * h + 3)
                    need(pe, s_q_l, h - 1)
                    for it in range(IT):
                        cols = slice(it * P, (it + 1) * P)
                        for k, (a, b) in enumerate(((wqn_h, wkb_h), (wqn_h, wkb_l), (wqn_l, wkb_h))):
                            mm = pe.matmul(p_q[p][:, it, :], a[p][:, cols], b[p][:, 0, :], start=(k == 0), stop=(k == 2))
                    mm.then_inc(s_q, 1)
                    need(pe, s_woT_l, h + 1)
                    need(pe, s_v_l, h - 1)
                    for k, (a, b) in enumerate(((wkb_h, woT_h), (wkb_h, woT_l), (wkb_l, woT_h))):
                        mm = pe.matmul(p_v[p][:, :], a[p][:, 1, :], b[p][:, :], start=(k == 0), stop=(k == 2))
                    mm.then_inc(s_v, 1)

            pair(0)
            with nc.Fori(1, H // 2, engines=[ENG.PE]) as m:
                pair(m)


def build_attention(nc, t, keep):
    with ExitStack() as ctx:
        def sb(name, shape, dt=F32):
            return ctx.enter_context(nc.sbuf_tensor(name, shape, dt))

        def ps(name, shape=(P, 512)):
            return ctx.enter_context(nc.psum_tensor(name, list(shape), F32))

        def sem(name):
            return ctx.enter_context(nc.semaphore(name))

        xT = sb("xT", [P, 2, IT, CW], F32R)
        acc = [sb(f"acc{i}_att", [P, QB, D]) for i in range(2)]
        cosT = sb("cosT_sb", [P, CW])
        sinT = sb("sinT_sb", [P, CW])
        Wq = [sb(f"Wq{i}", [P, 4, IT, P], F32R) for i in range(2)]
        Wv = [sb(f"Wv{i}", [P, 2, D], F32R) for i in range(2)]
        q_h = [sb(f"q_h{i}", [P, CW], F32R) for i in range(2)]
        q_l = [sb(f"q_l{i}", [P, CW], F32R) for i in range(2)]
        qp_h = [sb(f"qp_h{i}", [P, CW], F32R) for i in range(2)]
        qp_l = [sb(f"qp_l{i}", [P, CW], F32R) for i in range(2)]
        probs = [sb(f"probs{i}", [P, QB, S]) for i in range(2)]
        pT_h = [sb(f"pT_h{i}", [P, CW], F32R) for i in range(PT_RING)]
        pT_l = [sb(f"pT_l{i}", [P, CW], F32R) for i in range(PT_RING)]
        o_h = sb("o_h", [P, CW], F32R)
        o_l = sb("o_l", [P, CW], F32R)
        rot_cos = sb("rot_cos", [P, CW])
        rot_sin = sb("rot_sin", [P, CW])
        rotated = sb("rotated", [P, CW])
        part_max = [sb(f"part_max{i}", [P, QB, NCH]) for i in range(2)]
        neg_max = [sb(f"neg_max{i}", [P, QB]) for i in range(2)]
        row_sum = [sb(f"row_sum{i}", [P, QB]) for i in range(2)]
        inv_sum = [sb(f"inv_sum{i}", [P, QB]) for i in range(2)]
        ident, ident16, mask = keep["ident"], keep["ident16"], keep["mask"]
        Kn_h, Kn_l, Kp, V_h, V_l = (keep[k] for k in ("Kn_h", "Kn_l", "Kp", "V_h", "V_l"))

        p_score = [ps(f"p_score{i}") for i in range(2)]
        p_tr = [ps(f"p_tr{i}") for i in range(PT_RING)]
        p_out = ps("p_out")
        p_lat = ps("p_lat")
        p_rot = ps("p_rot")

        chunk_in = sem("chunk_in")
        wq_in = [sem(f"wq_in{i}") for i in range(2)]
        wv_in = [sem(f"wv_in{i}") for i in range(2)]
        result_out = sem("result_out")
        pe_projected = sem("pe_projected")
        lat_projected = sem("lat_projected")
        scored = sem("scored")
        transposed = sem("transposed")
        pv_done = sem("pv_done")
        out_projected = sem("out_projected")
        copied = sem("copied")
        maxed = sem("maxed")
        rot_read = sem("rot_read")
        rot_first = sem("rot_first")
        pT_split = sem("pT_split")
        o_split = sem("o_split")
        q_split = sem("q_split")
        inverted = sem("inverted")
        accumulated = sem("accumulated")
        exped = sem("exped")
        pT_high = sem("pT_high")
        o_high = sem("o_high")
        q_high = sem("q_high")
        qp_high = sem("qp_high")
        rot_added = sem("rot_added")
        qp_ready = sem("qp_ready")

        block = ctx.enter_context(nc.Block())
        result = t["out"].rearrange("(c a p) o -> c p a o", a=QB, p=P)

        @block.sync
        def _(sp):
            def load_q(pos):
                need(sp, pe_projected, heads_before(pos) - 1)
                need(sp, lat_projected, heads_before(pos) - 1)
                sp.dma_start(Wq[pos[2]][:, :, :, :].bitcast(F32), t["wq_scr"][2 * pos[1] + pos[2]]).then_inc(wq_in[pos[2]], 16)

            def load_v(pos):
                need(sp, out_projected, QB * (heads_before(pos) - 1))
                sp.dma_start(Wv[pos[2]][:, :, :].bitcast(F32), t["wv_scr"][2 * pos[1] + pos[2]]).then_inc(wv_in[pos[2]], 16)

            def load_chunk(j):
                need(sp, lat_projected, H * j)
                need(sp, pe_projected, H * j)
                sp.dma_start(xT[:, 0, :, :].bitcast(F32), t["xT_scr"][j, 0]).then_inc(chunk_in, 16)
                sp.dma_start(xT[:, 1, :, :].bitcast(F32), t["xT_scr"][j, 1]).then_inc(chunk_in, 16)
                need(sp, rot_read, H * j)
                sp.dma_start(cosT[:, :], t["cosT"][j]).then_inc(chunk_in, 16)
                sp.dma_start(sinT[:, :], t["sinT"][j]).then_inc(chunk_in, 16)
                if j >= 2:
                    sp.wait_ge(result_out, 16 * (j - 1))
                sp.dma_start(acc[j % 2][:, :, :], t["acc_scr"][j]).then_inc(chunk_in, 16)

            def store_chunk(j):
                sp.wait_ge(accumulated, QB * H * (j + 1))
                sp.dma_start(result[j], acc[j % 2][:, :, :]).then_inc(result_out, 16)

            for j in range(NCH):
                load_chunk(j)
                for p in range(2):
                    load_q((j, 0, p))
                    load_v((j, 0, p))
                if j >= 1:
                    store_chunk(j - 1)
                with nc.Fori(1, H // 2, engines=[ENG.SP]) as m:
                    for p in range(2):
                        load_q((j, m, p))
                        load_v((j, m, p))
            store_chunk(NCH - 1)
            sp.wait_ge(result_out, 16 * NCH)

        @block.tensor
        def _(pe):
            def project_rotary(pos):
                g, p = heads_before(pos), pos[2]
                pe.wait_ge(wq_in[p], 16 * (same_parity_before(pos) + 1))
                if first_of_chunk(pos):
                    pe.wait_ge(chunk_in, 80 * (pos[0] + 1))
                need(pe, rot_read, g)
                need(pe, accumulated, QB * (g - 2))
                product(p_rot[:, :], Wq[p][:, 2], Wq[p][:, 3], pe_projected)

            def project_latent(pos):
                g, p = heads_before(pos), pos[2]
                need(pe, q_split, g)
                need(pe, accumulated, QB * (g - 2))
                product(p_lat[:, :], Wq[p][:, 0], Wq[p][:, 1], lat_projected)

            def product(out, w_h, w_l, done):
                for it in range(IT):
                    for k, (w, x) in enumerate(((w_h, 0), (w_h, 1), (w_l, 0))):
                        mm = pe.matmul(out, w[:, it, :], xT[:, x, it, :], start=(it == 0 and k == 0),
                                       stop=(it == IT - 1 and k == 2))
                mm.then_inc(done, 1)

            def scores(pos, u):
                j, p = pos[0], pos[2]
                i, b = u // (j + 1), u % (j + 1)
                width = P * (i + 1) if b == j else CW
                if u == 0:
                    pe.wait_ge(q_split, heads_before(pos) + 1)
                    pe.wait_ge(qp_ready, heads_before(pos) + 1)
                need(pe, copied, tiles_before(pos) + u - 1)
                rows, keys = slice(i * P, (i + 1) * P), slice(b * CW, b * CW + width)
                out = p_score[u % 2]
                for k, (q, kk) in enumerate(((q_h, Kn_h), (q_h, Kn_l), (q_l, Kn_h), (qp_h, Kp), (qp_l, Kp))):
                    mm = pe.matmul(out[:, 0:width], q[p][:, rows], kk[:, keys], start=(k == 0),
                                   stop=(k == 4 and b < j))
                if b == j:
                    mm = pe.matmul(out[:, width - P:width], ident16[:, :], mask[:, :], start=False, stop=True)
                mm.then_inc(scored, 1)

            def transposes(pos, k):
                n, p = tiles_before(pos), pos[2]
                if k == 0:
                    pe.wait_ge(exped, rows_before(pos) + QB)
                need(pe, pT_split, n + k - PT_RING + 1 if k >= PT_RING else n)
                for i in range(first_row(pos, k), QB):
                    mm = pe.transpose(p_tr[k % PT_RING][:, i * P:(i + 1) * P], probs[p][:, i, k * P:(k + 1) * P],
                                      ident[:, :])
                mm.then_inc(transposed, 1)

            def values(pos, k):
                if k == 0:
                    need(pe, o_split, heads_before(pos))
                pe.wait_ge(pT_split, tiles_before(pos) + k + 1)
                cols, r = slice(first_row(pos, k) * P, CW), k % PT_RING
                last = k == tiles_of(pos) - 1
                for a, (v, pt) in enumerate(((V_h, pT_h), (V_h, pT_l), (V_l, pT_h))):
                    mm = pe.matmul(p_out[:, cols], v[:, k, :], pt[r][:, cols], start=(k == 0 and a == 0),
                                   stop=(last and a == 2))
                mm.then_inc(pv_done, 1)

            def project_out(pos, i, nxt):
                g, p = heads_before(pos), pos[2]
                if i == 0:
                    pe.wait_ge(o_split, g + 1)
                    pe.wait_ge(wv_in[p], 16 * (same_parity_before(pos) + 1))
                    pe.wait_ge(rot_read, heads_before(nxt) + 1 if nxt else NCH * H)
                    need(pe, accumulated, QB * g)
                elif i == 1:
                    pe.wait_ge(q_split, heads_before(nxt) + 1 if nxt else NCH * H)
                else:
                    pe.wait_ge(accumulated, QB * g + i - 1)
                out, rows = (p_rot, p_lat)[i % 2], slice(i * P, (i + 1) * P)
                for k, (o, w) in enumerate(((o_h, 0), (o_h, 1), (o_l, 0))):
                    mm = pe.matmul(out[:, :], o[:, rows], Wv[p][:, w, :], start=(k == 0), stop=(k == 2))
                mm.then_inc(out_projected, 1)

            def step(cur, prev, nxt):
                units = tiles_of(cur) if cur else tiles_of(prev)
                tiles = tiles_of(prev) if prev else 0
                done = 0
                for u in range(units):
                    if cur:
                        scores(cur, u)
                    if u < tiles:
                        transposes(prev, u)
                    if u >= 2 and u - 2 < tiles:
                        values(prev, u - 2)
                        done = u - 1
                if nxt:
                    project_rotary(nxt)
                for k in range(done, tiles):
                    values(prev, k)
                if nxt:
                    project_latent(nxt)
                if prev:
                    for i in range(QB):
                        project_out(prev, i, nxt)

            project_rotary((0, 0, 0))
            project_latent((0, 0, 0))
            walk(nc, ENG.PE, step)

        @block.vector
        def _(dve):
            def copy_scores(pos, u):
                j, p = pos[0], pos[2]
                i, b = u // (j + 1), u % (j + 1)
                width = P * (i + 1) if b == j else CW
                n = tiles_before(pos) + u
                dve.wait_ge(scored, n + 1)
                dve.tensor_scalar(probs[p][:, i, b * CW:b * CW + width], p_score[u % 2][:, 0:width], SCALE, LOWEST,
                                  ALU.mult, ALU.max, accum_out=part_max[p][:, i, b:b + 1]).then_inc(copied, 1)
                if b == j:
                    dve.wait_ge(copied, n + 1)
                    need(dve, exped, rows_before(pos) - QB)
                    dve.tensor_reduce(neg_max[p][:, i:i + 1], part_max[p][:, i, 0:j + 1], AXX, ALU.max,
                                      negate=True).then_inc(maxed, 1)

            def split_tile(pos, k):
                r, cols = k % PT_RING, slice(first_row(pos, k) * P, CW)
                dve.wait_ge(pT_high, tiles_before(pos) + k + 1)
                dve.tensor_tensor(pT_l[r][:, cols], p_tr[r][:, cols], pT_h[r][:, cols].bitcast(F32),
                                  ALU.subtract).then_inc(pT_split, 1)

            def rotate(pos):
                g = heads_before(pos)
                if first_of_chunk(pos):
                    dve.wait_ge(chunk_in, 80 * (pos[0] + 1))
                dve.wait_ge(pe_projected, g + 1)
                need(dve, rot_added, g)
                dve.tensor_tensor(rot_cos[:, :], p_rot[:, :], cosT[:, :], ALU.mult).then_inc(rot_first, 1)
                dve.tensor_tensor(rot_sin[0:64, :], p_rot[64:128, :], sinT[64:128, :], ALU.mult).then_inc(rot_first, 1)
                dve.tensor_tensor(rot_sin[64:128, :], p_rot[0:64, :], sinT[0:64, :], ALU.mult).then_inc(rot_read, 1)

            def split_query(pos):
                p = pos[2]
                dve.wait_ge(q_high, heads_before(pos) + 1)
                dve.tensor_tensor(q_l[p][:, :], p_lat[:, :], q_h[p][:, :].bitcast(F32), ALU.subtract).then_inc(q_split, 1)

            def split_output(pos):
                dve.wait_ge(o_high, heads_before(pos) + 1)
                dve.tensor_tensor(o_l[:, :], p_out[:, :], o_h[:, :].bitcast(F32), ALU.subtract).then_inc(o_split, 1)

            def accumulate(pos):
                g, p = heads_before(pos), pos[2]
                a = acc[pos[0] % 2]
                dve.wait_ge(exped, rows_before(pos) + QB)
                need(dve, accumulated, QB * g)
                dve.reciprocal(inv_sum[p][:, :], row_sum[p][:, :]).then_inc(inverted, 1)
                dve.wait_ge(inverted, g + 1)
                for i in range(QB):
                    dve.wait_ge(out_projected, QB * g + i + 1)
                    dve.scalar_tensor_tensor(out=a[:, i, :], in0=(p_rot, p_lat)[i % 2][:, :],
                                             scalar=inv_sum[p][:, i:i + 1], in1=a[:, i, :],
                                             op0=ALU.mult, op1=ALU.add).then_inc(accumulated, 1)

            def step(cur, prev, nxt):
                units = tiles_of(cur) if cur else tiles_of(prev)
                tiles = tiles_of(prev) if prev else 0
                for u in range(units):
                    if cur:
                        copy_scores(cur, u)
                    if u < tiles:
                        split_tile(prev, u)
                if nxt:
                    rotate(nxt)
                if prev:
                    split_output(prev)
                if nxt:
                    split_query(nxt)
                if prev:
                    accumulate(prev)

            rotate((0, 0, 0))
            split_query((0, 0, 0))
            walk(nc, ENG.DVE, step)

        @block.scalar
        def _(act):
            def exp_row(pos, i):
                p, width = pos[2], P * (QB * pos[0] + i + 1)
                act.wait_ge(maxed, rows_before(pos) + i + 1)
                need(act, inverted, heads_before(pos) - 1)
                act.activation(probs[p][:, i, 0:width], probs[p][:, i, 0:width], ACT.Exp,
                               bias=neg_max[p][:, i:i + 1], scale=1.0,
                               accum_out=row_sum[p][:, i:i + 1]).then_inc(exped, 1)

            def high_tile(pos, k):
                r, cols, n = k % PT_RING, slice(first_row(pos, k) * P, CW), tiles_before(pos)
                act.wait_ge(transposed, n + k + 1)
                need(act, pv_done, n + k - PT_RING + 1 if k >= PT_RING else n)
                act.activation(pT_h[r][:, cols], p_tr[r][:, cols], ACT.Copy).then_inc(pT_high, 1)

            def high_output(pos):
                g = heads_before(pos)
                act.wait_ge(pv_done, tiles_before(pos) + tiles_of(pos))
                need(act, out_projected, QB * g)
                act.activation(o_h[:, :], p_out[:, :], ACT.Copy).then_inc(o_high, 1)

            def high_query(pos):
                act.wait_ge(lat_projected, heads_before(pos) + 1)
                free_query(pos)
                act.activation(q_h[pos[2]][:, :], p_lat[:, :], ACT.Copy).then_inc(q_high, 1)

            def high_rotary(pos):
                act.wait_ge(rot_added, heads_before(pos) + 1)
                free_query(pos)
                act.activation(qp_h[pos[2]][:, :], rotated[:, :], ACT.Copy).then_inc(qp_high, 1)

            def free_query(pos):
                j, m, p = pos
                if first_of_chunk(pos):
                    need(act, scored, tiles_before((j - 1, H // 2 - 1, 1)) if j else 0)
                else:
                    need(act, scored, tiles_before((j, m, 0)) if p else tiles_before((j, m - 1, 1)))

            def step(cur, prev, nxt):
                units = tiles_of(cur) if cur else tiles_of(prev)
                tiles = tiles_of(prev) if prev else 0
                for u in range(units):
                    if u < tiles:
                        high_tile(prev, u)
                    if cur and (u + 1) % (cur[0] + 1) == 0:
                        exp_row(cur, u // (cur[0] + 1))
                if prev:
                    high_output(prev)
                if nxt:
                    high_query(nxt)
                    high_rotary(nxt)

            high_query((0, 0, 0))
            high_rotary((0, 0, 0))
            walk(nc, ENG.Activation, step)

        @block.gpsimd
        def _(pool):
            def rotary(pos):
                g, p = heads_before(pos), pos[2]
                pool.wait_ge(rot_read, g + 1)
                pool.wait_ge(rot_first, 2 * g + 2)
                need(pool, qp_ready, g)
                pool.tensor_tensor(rotated[:, :], rot_cos[:, :], rot_sin[:, :], ALU.add).then_inc(rot_added, 1)
                pool.wait_ge(qp_high, g + 1)
                pool.tensor_tensor(qp_l[p][:, :], rotated[:, :], qp_h[p][:, :].bitcast(F32),
                                   ALU.subtract).then_inc(qp_ready, 1)

            def step(cur, prev, nxt):
                if nxt:
                    rotary(nxt)

            rotary((0, 0, 0))
            walk(nc, ENG.Pool, step)


def build(nc, t):
    with ExitStack() as ctx:
        def sb(name, shape, dt=F32):
            return ctx.enter_context(nc.sbuf_tensor(name, shape, dt))

        keep = {
            "ident": sb("ident", [P, P]),
            "ident16": sb("ident16", [P, P], BF16),
            "mask": sb("mask_bf16", [P, P], BF16),
            "mask_f32": sb("mask_f32", [P, P]),
            "dup_f32": sb("dup_f32", [ROPE, P]),
            "Kn_h": sb("Kn_h", [P, S], F32R),
            "Kn_l": sb("Kn_l", [P, S], F32R),
            "Kp": sb("Kp", [P, S], F32R),
            "V_h": sb("V_h", [P, NT, RANK], F32R),
            "V_l": sb("V_l", [P, NT, RANK], F32R),
        }
        build_tokens(nc, t, keep)
        build_weights(nc, t, keep)
        build_attention(nc, t, keep)


def constants():
    freqs = 1.0 / 10000.0 ** (np.arange(0, ROPE, 2, dtype=np.float32) / ROPE)
    ang = np.outer(np.arange(S, dtype=np.float32), freqs)
    cos, sin = np.cos(ang), np.sin(ang)
    by_token = lambda a: np.ascontiguousarray(np.concatenate([a, a], 1).reshape(NT, P, ROPE).transpose(1, 0, 2))
    by_chunk = lambda a: np.ascontiguousarray(a.T.reshape(P, NCH, CW).transpose(1, 0, 2))
    dup = np.zeros((ROPE, P), np.float32)
    for x in range(2):
        for d in range(2):
            for f in range(HALF):
                dup[2 * f + x, ROPE * x + HALF * d + f] = 1.0
    return {
        "ident": np.eye(P, dtype=np.float32),
        "mask": np.where(np.tril(np.ones((P, P), bool)), 0.0, MASKED).astype(np.float32),
        "dup": dup,
        "cosN": by_token(cos),
        "sinN": by_token(sin),
        "cosT": by_chunk(np.concatenate([cos] * 4, 1)),
        "sinT": by_chunk(np.concatenate([sin, sin, -sin, -sin], 1)),
    }


_INS = {"x": "L0_attn_x", "wq": "L0_attn_wq", "wkv_a": "L0_attn_wkv_a", "wkv_b": "L0_attn_wkv_b",
        "wo": "L0_attn_wo", "kv_norm_w": "L0_attn_kv_norm_w", "w_ffn": "L0_ffn_weight", "b_ffn": "L0_ffn_bias"}


def kernel(**inputs):
    import concourse.bacc as bacc
    from concourse.bass_utils import run_bass_kernel_spmd

    arrays = {name: np.ascontiguousarray(inputs[key]) for name, key in _INS.items()}
    arrays["x"] = arrays["x"].reshape(S, D)
    arrays.update(constants())
    nc = bacc.Bacc("TRN2", target_bir_lowering=False, num_devices=1)
    t, feeds = {}, {}
    for name, a in arrays.items():
        t[name] = nc.dram_tensor(f"in_{name}", a.shape, F32, kind="ExternalInput").ap()
        feeds[f"in_{name}"] = a
    t["out"] = nc.dram_tensor("out_0", (S, D), F32, kind="ExternalOutput").ap()
    for name, shape, dt in (("xT_scr", (NCH, 2, P, IT, CW), F32), ("acc_scr", (NCH, P, QB, D), F32),
                            ("wq_scr", (H, P, 4, IT, P), F32), ("wv_scr", (H, P, 2, D), F32)):
        t[name] = nc.dram_tensor(name, shape, dt, kind="Internal").ap()
    build(nc, t)
    r = run_bass_kernel_spmd(nc, [feeds], core_ids=[0])
    return r.results[0]["out_0"].reshape(1, S, D)
```

```python
from contextlib import ExitStack

import numpy as np

import concourse.bass as bass
from concourse import mybir

ALU = mybir.AluOpType
ACT = mybir.ActivationFunctionType
AXX = mybir.AxisListType.X
F32 = mybir.dt.float32
F32R = mybir.dt.float32r
BF16 = mybir.dt.bfloat16
ENG = mybir.EngineType

P = 128
S = 2048
D = 512
H = 16
NOPE = 128
ROPE = 64
HALF = ROPE // 2
RANK = 128
VDIM = 128
QK = NOPE + ROPE
IT = D // P
CW = 512
NCH = S // CW
QB = CW // P
NT = S // P
SCALE = float(QK) ** -0.5
MASKED = -1.0e30
LN_EPS = 1e-5
RMS_EPS = 1e-6
FFN_EPS = 1e-10
LOWEST = -3.0e38
PT_RING = 3


def need(eng, sem, value):
    if isinstance(value, int) and value <= 0:
        return
    eng.wait_ge(sem, value)


def heads_before(pos):
    j, m, p = pos
    return H * j + 2 * m + p


def tiles_before(pos):
    j, m, p = pos
    return QB * H * (j * (j + 1) // 2) + QB * (j + 1) * (2 * m + p)


def rows_before(pos):
    return QB * heads_before(pos)


def pairs_before(pos):
    j, m, p = pos
    return (H // 2) * j + m


def tiles_of(pos):
    return QB * (pos[0] + 1)


def first_of_chunk(pos):
    return isinstance(pos[1], int) and pos[1:] == (0, 0)


def first_row(pos, k):
    return max(0, k - QB * pos[0])


def walk(nc, engine, step):
    def two_steps(j, m):
        step((j, m, 1), (j, m, 0), (j, m + 1, 0))
        step((j, m + 1, 0), (j, m, 1), (j, m + 1, 1))

    for j in range(NCH):
        step((j, 0, 0), (j - 1, H // 2 - 1, 1) if j else None, (j, 0, 1))
        if j == 0:
            two_steps(0, 0)
        with nc.Fori(0 if j else 1, H // 2 - 1, engines=[engine]) as m:
            two_steps(j, m)
        step((j, H // 2 - 1, 1), (j, H // 2 - 1, 0), (j + 1, 0, 0) if j + 1 < NCH else None)
    step(None, (NCH - 1, H // 2 - 1, 1), None)


def build_prepare(nc, t, keep):
    with ExitStack() as ctx:
        def sb(name, shape, dt=F32):
            return ctx.enter_context(nc.sbuf_tensor(name, shape, dt))

        def ps(name, shape):
            return ctx.enter_context(nc.psum_tensor(name, shape, F32))

        def sem(name):
            return ctx.enter_context(nc.semaphore(name))

        ident, xT, residual = keep["ident"], keep["xT"], keep["acc0"]
        Wq, Wp, Wv = keep["Wq"], keep["Wp"], keep["Wv"]
        w_ffn = sb("w_ffn", [P, IT, D])
        ffnT_h = sb("ffnT_h", [P, IT, D], F32R)
        ffnT_l = sb("ffnT_l", [P, IT, D], F32R)
        w_kva = sb("w_kva", [96, 2, D])
        kvaT_h = sb("kvaT_h", [P, IT, 192], F32R)
        kvaT_l = sb("kvaT_l", [P, IT, 192], F32R)
        rows = sb("rows", [1, D + RANK])
        ones = sb("ones", [P, P])
        bias_all = sb("bias_all", [P, D])
        norm_all = sb("norm_all", [P, RANK])
        wsum = sb("wsum", [P, 8])
        minus_half = sb("minus_half", [P, QB])
        x_in = sb("x_in", [P, QB, D])
        xhat = sb("xhat", [P, QB, D])
        xb = sb("xb", [P, QB, D])
        stats = sb("stats", [P, QB, 6])
        moments = sb("moments", [P, QB, 2])
        var_eps = sb("var_eps", [P, QB])
        rstd = sb("rstd", [P, QB])
        squares = sb("squares", [P, RANK])
        sumsq = sb("sumsq", [P, QB])
        ms = sb("ms", [P, QB])
        rrms = sb("rrms", [P, QB])
        lat = sb("lat", [P, QB, RANK])
        by_cos = sb("by_cos", [P, QB, ROPE])
        by_sin = sb("by_sin", [P, QB, ROPE])
        roped = sb("roped", [P, QB, ROPE])
        kpe = sb("kpe", [P, QB, 2, ROPE], F32R)
        cosN = sb("cosN_sb", [P, NT * ROPE])
        sinN = sb("sinN_sb", [P, NT * ROPE])
        wqn = [sb(f"wqn{i}", [P, D]) for i in range(2)]
        wqn_h = [sb(f"wqn_h{i}", [P, D], F32R) for i in range(2)]
        wqn_l = [sb(f"wqn_l{i}", [P, D], F32R) for i in range(2)]
        wqp = sb("wqp", [P, D])
        wqp_h = sb("wqp_h", [P, D], F32R)
        wqp_l = sb("wqp_l", [P, D], F32R)
        order = sb("order", [P, ROPE], F32R)
        wkb = [sb(f"wkb{i}", [P, 2, RANK]) for i in range(2)]
        wkb_h = [sb(f"wkb_h{i}", [P, 2, RANK], F32R) for i in range(2)]
        wkb_l = [sb(f"wkb_l{i}", [P, 2, RANK], F32R) for i in range(2)]
        wo = [sb(f"wo{i}", [P, IT, VDIM]) for i in range(2)]
        woT_h = sb("woT_h", [P, D], F32R)
        woT_l = sb("woT_l", [P, D], F32R)
        w_flat = w_ffn[:, :, :].rearrange("p a i -> p (a i)")
        w_pos = residual[:, :, :].rearrange("p a i -> p (a i)")
        w_neg = xb[:, :, :].rearrange("p a i -> p (a i)")
        w_tern = xhat[:, :, :].rearrange("p a i -> p (a i)")
        w_ste = xb

        pX = [ps(f"pX{i}", [P, IT, P]) for i in range(2)]
        pKV = [ps(f"pKV{i}", [P, 512]) for i in range(2)]
        pF = ps("pF", [P, D])
        pK = ps("pK", [P, 4, P])
        pW = [ps(f"pW{i}", [P, 512]) for i in range(2)]
        pQ = pW[0][:, :].rearrange("p (a c) -> p a c", a=IT)
        pP = pW[1][:, :].rearrange("p (k a c) -> p k a c", k=2, a=IT)
        p_ffn = [pF, pW[1]]

        s_const = sem("s_const")
        s_tables = sem("s_tables")
        s_w = sem("s_w")
        s_ones = sem("s_ones")
        s_bcast = sem("s_bcast")
        s_bcast_out = sem("s_bcast_out")
        s_abs = sem("s_abs")
        s_total = sem("s_total")
        s_thr = sem("s_thr")
        s_tern = sem("s_tern")
        s_wT = sem("s_wT")
        s_wT_h = sem("s_wT_h")
        s_wT_l = sem("s_wT_l")
        s_aT = sem("s_aT")
        s_aT_h = sem("s_aT_h")
        s_aT_l = sem("s_aT_l")
        s_x = sem("s_x")
        s_stats = sem("s_stats")
        s_moments = sem("s_moments")
        s_var = sem("s_var")
        s_rstd = sem("s_rstd")
        s_xhat = sem("s_xhat")
        s_xb = sem("s_xb")
        s_xT = sem("s_xT")
        s_xT_h = sem("s_xT_h")
        s_xT_l = sem("s_xT_l")
        s_kv = sem("s_kv")
        s_sumsq = sem("s_sumsq")
        s_ms = sem("s_ms")
        s_rrms = sem("s_rrms")
        s_rot = sem("s_rot")
        s_lat = sem("s_lat")
        s_roped = sem("s_roped")
        s_vh = sem("s_vh")
        s_kpe_h = sem("s_kpe_h")
        s_kpe_l = sem("s_kpe_l")
        s_ffn = sem("s_ffn")
        s_acc = sem("s_acc")
        s_kT = sem("s_kT")
        s_kT_h = sem("s_kT_h")
        s_kT_l = sem("s_kT_l")
        s_xT_out = sem("s_xT_out")
        s_acc_out = sem("s_acc_out")
        s_load = [sem(f"s_load{i}") for i in range(2)]
        s_order = sem("s_order")
        s_high = sem("s_high")
        s_low = sem("s_low")
        s_woT = sem("s_woT")
        s_woT_h = sem("s_woT_h")
        s_woT_l = sem("s_woT_l")
        s_pe = sem("s_pe")
        s_pe_h = sem("s_pe_h")
        s_pe_l = sem("s_pe_l")
        s_q = sem("s_q")
        s_q_h = sem("s_q_h")
        s_q_l = sem("s_q_l")
        s_v = sem("s_v")
        s_v_h = sem("s_v_h")
        s_v_l = sem("s_v_l")
        s_wq_out = [sem(f"s_wq_out{i}") for i in range(2)]
        s_wv_out = [sem(f"s_wv_out{i}") for i in range(2)]
        s_wp_out = sem("s_wp_out")

        block = ctx.enter_context(nc.Block())
        wq_heads = t["wq"].rearrange("(h r) i -> h r i", h=H)
        wkb_heads = t["wkv_b"].rearrange("(h two d) c -> h d two c", h=H, two=2)
        wo_heads = t["wo"].rearrange("(a p) (h d) -> h p a d", p=P, h=H)
        x_chunks = t["x"].rearrange("(c a p) i -> c p a i", a=QB, p=P)

        def rounds(engine, round_):
            round_(0, True)
            with nc.Fori(1, NCH - 1, engines=[engine]) as c:
                round_(c, True)
            round_(NCH - 1, False)

        def at(tensor, c, b, n=1):
            return tensor[:, bass.ds(c * (-n * QB) + n * (QB * (NCH - 1) + b), n)]

        @block.sync
        def _(sp):
            def load_head(c, k):
                h, i = c * -QB + (H - 1 - k), k % 2
                sp.dma_start(wqp[ROPE * i:ROPE * (i + 1), :], wq_heads[h][NOPE:QK, :]).then_inc(s_load[i], 16)
                sp.dma_start(wkb[i][:, :, :], wkb_heads[h]).then_inc(s_load[i], 16)
                sp.dma_start(wqn[i][:, :], wq_heads[h][0:NOPE, :]).then_inc(s_load[i], 16)
                sp.dma_start(wo[i][:, :, :], wo_heads[h]).then_inc(s_load[i], 16)

            sp.dma_start(w_ffn[:, :, :], t["w_ffn"].rearrange("(a p) i -> p a i", p=P)).then_inc(s_w, 16)
            sp.dma_start(ident[:, :], t["ident"]).then_inc(s_const, 16)
            sp.dma_start(rows[:, 0:D], t["b_ffn"].rearrange("(a n) -> a n", a=1)).then_inc(s_const, 16)
            sp.dma_start(rows[:, D:], t["kv_norm_w"].rearrange("(a n) -> a n", a=1)).then_inc(s_const, 16)
            sp.dma_start(w_kva[:, :, :], t["wkv_a"].rearrange("(a p) i -> p a i", p=96)).then_inc(s_const, 16)
            sp.dma_start(keep["order_f32"][:, :], t["order"]).then_inc(s_const, 16)
            sp.dma_start(keep["mask_f32"][:, :], t["mask"]).then_inc(s_const, 16)
            sp.dma_start(x_in[:, :, :], x_chunks[NCH - 1]).then_inc(s_x, 16)
            load_head(0, 0)
            load_head(0, 1)
            sp.dma_start(cosN[:, :], t["cosN"].rearrange("p n c -> p (n c)")).then_inc(s_tables, 16)
            sp.dma_start(sinN[:, :], t["sinN"].rearrange("p n c -> p (n c)")).then_inc(s_tables, 16)
            sp.dma_start(keep["cosT"][:, :], t["cosT"][0]).then_inc(s_tables, 16)
            sp.dma_start(keep["sinT"][:, :], t["sinT"][0]).then_inc(s_tables, 16)

            def round_(c, more):
                d = c * -1 + (NCH - 1)
                for k in range(QB):
                    n, h = QB * c + k, c * -QB + (H - 1 - k)
                    if more or k < 2:
                        sp.wait_ge(s_woT, n + 1)
                        sp.wait_ge(s_high, 3 * n + 3)
                        sp.wait_ge(s_low, 3 * n + 3)
                        load_head(c, k + 2)
                    if k == 0 and more:
                        sp.wait_ge(s_xhat, QB * (c + 1))
                        sp.wait_ge(s_xb, QB * (c + 1))
                        sp.dma_start(x_in[:, :, :], x_chunks[d - 1]).then_inc(s_x, 16)
                    if k == 1:
                        sp.wait_ge(s_xT_l, QB * (c + 1))
                        sp.dma_start(t["xT_scr"][d], xT[:, :, :, :].bitcast(F32)).then_inc(s_xT_out, 16)
                    sp.wait_ge(s_q_l, n + 1)
                    sp.dma_start(t["wq_scr"][h], Wq[1 - k % 2][:, :, :, :].bitcast(F32)).then_inc(s_wq_out[k % 2], 16)
                    sp.wait_ge(s_v_l, n + 1)
                    sp.dma_start(t["wv_scr"][h], Wv[1 - k % 2][:, :, :].bitcast(F32)).then_inc(s_wv_out[k % 2], 16)
                    if k % 2:
                        sp.wait_ge(s_pe_h, n + 1)
                        sp.wait_ge(s_pe_l, n + 1)
                        sp.dma_start(t["wp_scr"][c * -2 + (H // 2 - 1 - k // 2)],
                                     Wp[:, :, :, :].bitcast(F32)).then_inc(s_wp_out, 16)
                    if k == 2:
                        sp.wait_ge(s_acc, QB * (c + 1))
                        sp.dma_start(t["acc_scr"][d], residual[:, :, :]).then_inc(s_acc_out, 16)

            rounds(ENG.SP, round_)
            for i in range(2):
                sp.wait_ge(s_wq_out[i], 16 * H // 2)
                sp.wait_ge(s_wv_out[i], 16 * H // 2)
            sp.wait_ge(s_wp_out, 16 * H // 2)
            sp.wait_ge(s_xT_out, 16 * NCH)
            sp.wait_ge(s_acc_out, 16 * NCH)
            sp.wait_ge(s_tables, 64)

        @block.gpsimd
        def _(pool):
            def low_parts(c, k):
                n, i = QB * c + k, k % 2
                half = slice(ROPE * i, ROPE * (i + 1))
                pool.wait_ge(s_high, 3 * n + 1)
                pool.tensor_tensor(wkb_l[i][:, :, :], wkb[i][:, :, :], wkb_h[i][:, :, :].bitcast(F32),
                                   ALU.subtract).then_inc(s_low, 1)
                pool.wait_ge(s_high, 3 * n + 2)
                pool.wait_ge(s_low, 3 * n + 1)
                pool.tensor_tensor(wqp_l[half, :], wqp[half, :], wqp_h[half, :].bitcast(F32),
                                   ALU.subtract).then_inc(s_low, 1)
                pool.wait_ge(s_high, 3 * n + 3)
                pool.wait_ge(s_low, 3 * n + 2)
                pool.tensor_tensor(wqn_l[i][:, :], wqn[i][:, :], wqn_h[i][:, :].bitcast(F32),
                                   ALU.subtract).then_inc(s_low, 1)

            def norm(c):
                need(pool, s_var, c + 1)
                pool.tensor_tensor(rstd[:, :], var_eps[:, :], minus_half[:, :], ALU.pow).then_inc(s_rstd, 1)

            def add_bias(c):
                need(pool, s_acc, QB * c)
                pool.wait_ge(s_x, 16 * (c + 1))
                for b in range(QB):
                    pool.tensor_tensor(xb[:, b, :], x_in[:, b, :], bias_all[:, :], ALU.add).then_inc(s_xb, 1)

            def rotary_key(c, b):
                n = QB * c + b
                pool.wait_ge(s_ms, n + 1)
                pool.tensor_tensor(rrms[:, b:b + 1], ms[:, b:b + 1], minus_half[:, b:b + 1],
                                   ALU.pow).then_inc(s_rrms, 1)
                pool.wait_ge(s_rot, n + 1)
                need(pool, s_kpe_h, QB * c)
                pool.tensor_tensor(roped[:, b, 0:HALF], by_cos[:, b, 0:HALF], by_sin[:, b, HALF:], ALU.subtract)
                pool.tensor_tensor(roped[:, b, HALF:], by_cos[:, b, HALF:], by_sin[:, b, 0:HALF],
                                   ALU.add).then_inc(s_roped, 1)

            def low_keys(c, b):
                n = QB * c + b
                pool.wait_ge(s_kpe_h, n + 1)
                pool.tensor_tensor(kpe[:, b, 1, :], roped[:, b, :], kpe[:, b, 0, :].bitcast(F32),
                                   ALU.subtract).then_inc(s_kpe_l, 1)
                pool.wait_ge(s_vh, n + 1)
                pool.tensor_tensor(at(keep["V_l"], c, b, RANK), lat[:, b, :], at(keep["V_h"], c, b, RANK).bitcast(F32),
                                   ALU.subtract)

            pool.memset(minus_half[:, :], -0.5).then_inc(s_ones, 1)
            pool.wait_ge(s_ones, 2)
            low_parts(0, 0)
            norm(0)
            pool.wait_ge(s_bcast_out, 2)
            pool.wait_ge(s_wT, IT)
            add_bias(0)

            def round_(c, more):
                for s in range(4 * QB):
                    if s in (4, 5, 7, 9):
                        rotary_key(c, (4, 5, 7, 9).index(s))
                    if s in (6, 8, 10, 11):
                        low_keys(c, (6, 8, 10, 11).index(s))
                    if s == 11 and more:
                        norm(c + 1)
                    if s == 12 and more:
                        add_bias(c + 1)
                    if s % 4 == 2 and (more or s < 12):
                        low_parts(c, s // 4 + 1)

            rounds(ENG.Pool, round_)

        @block.scalar
        def _(act):
            def high_parts(c, k):
                n, i = QB * c + k, k % 2
                half = slice(ROPE * i, ROPE * (i + 1))
                act.wait_ge(s_load[i], 64 * (2 * c + k // 2 + 1))
                need(act, s_v, n - 1)
                act.activation(wkb_h[i][:, :, :], wkb[i][:, :, :], ACT.Copy).then_inc(s_high, 1)
                act.activation(wqp_h[half, :], wqp[half, :], ACT.Copy).then_inc(s_high, 1)
                act.activation(wqn_h[i][:, :], wqn[i][:, :], ACT.Copy).then_inc(s_high, 1)

            def weights(c, k, part):
                n, i = QB * c + k, k % 2
                if part == 0:
                    act.wait_ge(s_woT, n + 1)
                    need(act, s_v, n)
                    act.activation(woT_h[:, :], pW[0][:, :], ACT.Copy).then_inc(s_woT_h, 1)
                elif part == 1:
                    act.wait_ge(s_pe, n + 1)
                    if i == 0:
                        need(act, s_wp_out, 16 * (2 * c + k // 2))
                    act.activation(Wp[:, 0, :, ROPE * (1 - i):ROPE * (2 - i)], pP[:, 0, :, :],
                                   ACT.Copy).then_inc(s_pe_h, 1)
                elif part == 2:
                    act.wait_ge(s_q, n + 1)
                    need(act, s_wq_out[i], 16 * (2 * c + k // 2))
                    act.activation(Wq[1 - i][:, 0, :, :], pQ, ACT.Copy).then_inc(s_q_h, 1)
                else:
                    act.wait_ge(s_v, n + 1)
                    need(act, s_wv_out[i], 16 * (2 * c + k // 2))
                    act.activation(Wv[1 - i][:, 0, :], pW[1][:, :], ACT.Copy).then_inc(s_v_h, 1)

            def x_high(c, b):
                if b == 0:
                    need(act, s_xT_out, 16 * c)
                act.wait_ge(s_xT, QB * c + b + 1)
                act.activation(xT[:, 0, :, b * P:(b + 1) * P], pX[b % 2][:, :, :], ACT.Copy).then_inc(s_xT_h, 1)

            def square(c, b):
                n = QB * c + b
                act.wait_ge(s_kv, n + 1)
                need(act, s_sumsq, n)
                act.activation(squares[:, :], pKV[b % 2][:, 0:RANK], ACT.Square,
                               accum_out=sumsq[:, b:b + 1]).then_inc(s_sumsq, 1)

            def high_keys(c, b):
                n = QB * c + b
                act.wait_ge(s_roped, n + 1)
                need(act, s_kT, QB * c)
                act.activation(kpe[:, b, 0, :], roped[:, b, :], ACT.Copy).then_inc(s_kpe_h, 1)
                act.wait_ge(s_lat, n + 1)
                act.activation(at(keep["V_h"], c, b, RANK), lat[:, b, :], ACT.Copy).then_inc(s_vh, 1)

            def high_keys_transposed(c, b):
                act.wait_ge(s_kT, QB * c + b + 1)
                act.activation(at(keep["Kn_h"], c, b, P), pK[:, 0, :], ACT.Copy)
                act.activation(at(keep["Kp"], c, b, P), pK[:, 1, :], ACT.Copy).then_inc(s_kT_h, 1)

            act.wait_ge(s_const, 16 * 6)
            act.activation(keep["mask"][:, :], keep["mask_f32"][:, :], ACT.Copy)
            act.activation(keep["ident16"][:, :], ident[:, :], ACT.Copy)
            act.activation(order[:, :], keep["order_f32"][:, :], ACT.Copy).then_inc(s_order, 1)
            act.wait_ge(s_aT, 1)
            act.activation(kvaT_h[:, :, 0:96], pX[0][:, :, 0:96], ACT.Copy).then_inc(s_aT_h, 1)
            act.wait_ge(s_aT, 2)
            act.activation(kvaT_h[:, :, 96:128], pX[1][:, :, 0:32], ACT.Copy).then_inc(s_aT_h, 1)
            for x in range(2):
                act.activation(kvaT_h[:, :, 128 + HALF * x:128 + HALF * (x + 1)], pX[1][:, :, 32 + x:96:2],
                               ACT.Copy).then_inc(s_aT_h, 1)
            high_parts(0, 0)
            for it in range(IT):
                act.wait_ge(s_wT, it + 1)
                act.activation(ffnT_h[:, it, :], p_ffn[it % 2][:, :], ACT.Copy).then_inc(s_wT_h, 1)

            def round_(c, more):
                for s in range(4 * QB):
                    if s < 4:
                        x_high(c, s)
                    if s in (4, 5, 7, 9):
                        square(c, (4, 5, 7, 9).index(s))
                    if s in (6, 8, 10, 11):
                        high_keys(c, (6, 8, 10, 11).index(s))
                    if s >= 12:
                        high_keys_transposed(c, s - 12)
                    weights(c, s // 4, s % 4)
                    if s % 4 == 1 and (more or s < 12):
                        high_parts(c, s // 4 + 1)

            rounds(ENG.Activation, round_)

        @block.vector
        def _(dve):
            def normalise(c):
                dve.wait_ge(s_x, 16 * (c + 1))
                for b in range(QB):
                    dve.bn_stats(stats[:, b, :], x_in[:, b, :]).then_inc(s_stats, 4)
                dve.wait_ge(s_ones, 2)
                dve.wait_ge(s_stats, 16 * (c + 1))
                for b in range(QB):
                    dve.bn_aggr(moments[:, b, :], stats[:, b, :]).then_inc(s_moments, 1)
                dve.wait_ge(s_moments, QB * (c + 1))
                dve.tensor_scalar(var_eps[:, :], moments[:, :, 1], LN_EPS, None, ALU.add).then_inc(s_var, 1)

            def scale_x(c):
                dve.wait_ge(s_rstd, c + 1)
                need(dve, s_xT, QB * c)
                for b in range(QB):
                    dve.tensor_scalar(xhat[:, b, :], x_in[:, b, :], moments[:, b, 0:1], rstd[:, b:b + 1],
                                      ALU.subtract, ALU.mult).then_inc(s_xhat, 1)

            def x_low(c, b):
                cols = slice(b * P, (b + 1) * P)
                dve.wait_ge(s_xT_h, QB * c + b + 1)
                dve.tensor_tensor(xT[:, 1, :, cols], pX[b % 2][:, :, :], xT[:, 0, :, cols].bitcast(F32),
                                  ALU.subtract).then_inc(s_xT_l, 1)

            def linear(c, b):
                dve.wait_ge(s_ffn, QB * c + b + 1)
                dve.wait_ge(s_xb, QB * c + b + 1)
                if b == 0:
                    need(dve, s_acc_out, 16 * c)
                dve.tensor_tensor(residual[:, b, :], pF[:, :], xb[:, b, :], ALU.add).then_inc(s_acc, 1)

            def rotary_key(c, b):
                n = QB * c + b
                rotary = pKV[b % 2][:, RANK:RANK + ROPE]
                dve.wait_ge(s_sumsq, n + 1)
                need(dve, s_roped, QB * c)
                dve.tensor_tensor(by_cos[:, b, :], rotary, at(cosN, c, b, ROPE), ALU.mult)
                dve.tensor_tensor(by_sin[:, b, :], rotary, at(sinN, c, b, ROPE), ALU.mult).then_inc(s_rot, 1)
                need(dve, s_rrms, QB * c)
                dve.tensor_scalar(ms[:, b:b + 1], sumsq[:, b:b + 1], 1.0 / RANK, RMS_EPS,
                                  ALU.mult, ALU.add).then_inc(s_ms, 1)

            def latent_row(c, b):
                dve.wait_ge(s_rrms, QB * c + b + 1)
                need(dve, s_kT, QB * c)
                dve.scalar_tensor_tensor(out=lat[:, b, :], in0=pKV[b % 2][:, 0:RANK], scalar=rrms[:, b:b + 1],
                                         in1=norm_all[:, :], op0=ALU.mult, op1=ALU.mult).then_inc(s_lat, 1)

            def low_keys_transposed(c, b):
                dve.wait_ge(s_kT_h, QB * c + b + 1)
                dve.tensor_tensor(at(keep["Kn_l"], c, b, P), pK[:, 0, :], at(keep["Kn_h"], c, b, P).bitcast(F32),
                                  ALU.subtract).then_inc(s_kT_l, 1)

            def weights(c, k, part):
                n, i = QB * c + k, k % 2
                if part == 0:
                    dve.wait_ge(s_woT_h, n + 1)
                    dve.tensor_tensor(woT_l[:, :], pW[0][:, :], woT_h[:, :].bitcast(F32),
                                      ALU.subtract).then_inc(s_woT_l, 1)
                elif part == 1:
                    dve.wait_ge(s_pe_h, n + 1)
                    dve.tensor_copy(Wp[:, 1, :, ROPE * (1 - i):ROPE * (2 - i)], pP[:, 1, :, :]).then_inc(s_pe_l, 1)
                elif part == 2:
                    dve.wait_ge(s_q_h, n + 1)
                    dve.tensor_tensor(Wq[1 - i][:, 1, :, :], pQ, Wq[1 - i][:, 0, :, :].bitcast(F32),
                                      ALU.subtract).then_inc(s_q_l, 1)
                else:
                    dve.wait_ge(s_v_h, n + 1)
                    dve.tensor_tensor(Wv[1 - i][:, 1, :], pW[1][:, :], Wv[1 - i][:, 0, :].bitcast(F32),
                                      ALU.subtract).then_inc(s_v_l, 1)

            dve.memset(ones[:, :], 1.0).then_inc(s_ones, 1)
            dve.wait_ge(s_w, 16)
            dve.tensor_reduce(wsum[:, 0:1], w_flat, AXX, ALU.add, apply_absolute_value=True).then_inc(s_abs, 1)
            dve.wait_ge(s_total, 1)
            dve.tensor_scalar(wsum[:, 1:2], pK[:, 0, 0:1], 1.0 / (D * D), None, ALU.mult).then_inc(s_thr, 1)
            dve.wait_ge(s_thr, 1)
            dve.tensor_scalar(wsum[:, 2:3], wsum[:, 1:2], FFN_EPS, 0.5, ALU.add, ALU.mult).then_inc(s_thr, 1)
            dve.tensor_scalar(wsum[:, 4:5], wsum[:, 1:2], FFN_EPS, -0.5, ALU.add, ALU.mult).then_inc(s_thr, 1)
            dve.wait_ge(s_thr, 3)
            dve.tensor_scalar(w_pos, w_flat, wsum[:, 2:3], None, ALU.is_gt).then_inc(s_tern, 1)
            dve.tensor_scalar(w_neg, w_flat, wsum[:, 4:5], None, ALU.is_lt).then_inc(s_tern, 1)
            dve.wait_ge(s_tern, 2)
            dve.tensor_tensor(w_tern, w_pos, w_neg, ALU.subtract).then_inc(s_tern, 1)
            dve.wait_ge(s_tern, 3)
            dve.scalar_tensor_tensor(out=w_pos, in0=w_tern, scalar=wsum[:, 1:2], in1=w_flat,
                                     op0=ALU.mult, op1=ALU.subtract).then_inc(s_tern, 1)
            dve.wait_ge(s_tern, 4)
            dve.tensor_tensor(w_ste[:, :, :].rearrange("p a i -> p (a i)"), w_pos, w_flat, ALU.add).then_inc(s_tern, 1)
            dve.wait_ge(s_bcast, 2)
            dve.tensor_copy(bias_all[:, :], pKV[0][:, :]).then_inc(s_bcast_out, 1)
            dve.tensor_copy(norm_all[:, :], pKV[1][:, 0:RANK]).then_inc(s_bcast_out, 1)
            normalise(0)
            dve.wait_ge(s_aT_h, 4)
            dve.tensor_tensor(kvaT_l[:, :, 0:96], pX[0][:, :, 0:96], kvaT_h[:, :, 0:96].bitcast(F32), ALU.subtract)
            dve.tensor_tensor(kvaT_l[:, :, 96:128], pX[1][:, :, 0:32], kvaT_h[:, :, 96:128].bitcast(F32),
                              ALU.subtract)
            for x in range(2):
                cols = slice(128 + HALF * x, 128 + HALF * (x + 1))
                kva_low = dve.tensor_tensor(kvaT_l[:, :, cols], pX[1][:, :, 32 + x:96:2],
                                            kvaT_h[:, :, cols].bitcast(F32), ALU.subtract)
            kva_low.then_inc(s_aT_l, 1)
            scale_x(0)
            for it in range(IT):
                dve.wait_ge(s_wT_h, it + 1)
                dve.tensor_tensor(ffnT_l[:, it, :], p_ffn[it % 2][:, :], ffnT_h[:, it, :].bitcast(F32),
                                  ALU.subtract).then_inc(s_wT_l, 1)
            dve.wait_ge(s_tables, 64)

            def round_(c, more):
                for s in range(4 * QB):
                    if s < 4:
                        x_low(c, s)
                    if s in (5, 7, 9):
                        latent_row(c, (5, 7, 9).index(s))
                    if s in (4, 5, 7, 9):
                        rotary_key(c, (4, 5, 7, 9).index(s))
                    if s in (6, 8, 10, 11):
                        linear(c, (6, 8, 10, 11).index(s))
                    if s == 10:
                        latent_row(c, 3)
                    if s == 11 and more:
                        normalise(c + 1)
                    if s >= 12:
                        low_keys_transposed(c, s - 12)
                    weights(c, s // 4, s % 4)
                    if s == 12 and more:
                        scale_x(c + 1)

            rounds(ENG.DVE, round_)

        @block.tensor
        def _(pe):
            def transpose_x(c, b):
                n = QB * c + b
                pe.wait_ge(s_xhat, n + 1)
                if b >= 2:
                    pe.wait_ge(s_xT_l, n - 1)
                for it in range(IT):
                    mm = pe.transpose(pX[b % 2][:, it, :], xhat[:, b, it * P:(it + 1) * P], ident[:, :])
                mm.then_inc(s_xT, 1)

            def product(out, b, w_h, w_l, done):
                cols = slice(b * P, (b + 1) * P)
                for it in range(IT):
                    for k, (x, w) in enumerate(((0, w_h), (0, w_l), (1, w_h))):
                        mm = pe.matmul(out, xT[:, x, it, cols], w[:, it, :], start=(it == 0 and k == 0),
                                       stop=(it == IT - 1 and k == 2))
                mm.then_inc(done, 1)

            def latent(c, b):
                n = QB * c + b
                pe.wait_ge(s_xT_l, n + 1)
                need(pe, s_lat, n - 1)
                product(pKV[b % 2][:, 0:192], b, kvaT_h, kvaT_l, s_kv)

            def linear(c, b):
                need(pe, s_acc, QB * c + b)
                product(pF[:, :], b, ffnT_h, ffnT_l, s_ffn)

            def transpose_keys(c, b):
                n = QB * c + b
                need(pe, s_kT_l, n)
                pe.wait_ge(s_lat, n + 1)
                pe.transpose(pK[:, 0, :], lat[:, b, :], ident[:, :])
                pe.wait_ge(s_kpe_l, n + 1)
                pe.transpose(pK[:, 1, :], kpe[:, b, :, :].rearrange("p h f -> p (h f)").bitcast(F32),
                             ident[:, :]).then_inc(s_kT, 1)

            def weights(c, k, part):
                n, i = QB * c + k, k % 2
                if part == 0:
                    pe.wait_ge(s_load[i], 64 * (2 * c + k // 2 + 1))
                    need(pe, s_q_l, n)
                    for a in range(IT):
                        mm = pe.transpose(pW[0][:, a * P:(a + 1) * P], wo[i][:, a, :], ident[:, :])
                    mm.then_inc(s_woT, 1)
                elif part == 1:
                    half = slice(ROPE * i, ROPE * (i + 1))
                    pe.wait_ge(s_low, 3 * n + 2)
                    need(pe, s_v_l, n)
                    for x, w in enumerate((wqp_h, wqp_l)):
                        for it in range(IT):
                            mm = pe.matmul(pP[:, x, it, :], w[half, it * P:(it + 1) * P], order[half, :],
                                           start=True, stop=True)
                    mm.then_inc(s_pe, 1)
                elif part == 2:
                    pe.wait_ge(s_low, 3 * n + 3)
                    pe.wait_ge(s_woT_l, n + 1)
                    for it in range(IT):
                        cols = slice(it * P, (it + 1) * P)
                        for x, (a, b) in enumerate(((wqn_h, wkb_h), (wqn_h, wkb_l), (wqn_l, wkb_h))):
                            mm = pe.matmul(pQ[:, it, :], a[i][:, cols], b[i][:, 0, :], start=(x == 0), stop=(x == 2))
                    mm.then_inc(s_q, 1)
                else:
                    pe.wait_ge(s_pe_l, n + 1)
                    for x, (a, b) in enumerate(((wkb_h, woT_h), (wkb_h, woT_l), (wkb_l, woT_h))):
                        mm = pe.matmul(pW[1][:, :], a[i][:, 1, :], b[:, :], start=(x == 0), stop=(x == 2))
                    mm.then_inc(s_v, 1)

            pe.wait_ge(s_ones, 2)
            pe.wait_ge(s_const, 16 * 6)
            pe.matmul(pKV[0][:, :], ones[0:1, :], rows[:, 0:D], start=True, stop=True).then_inc(s_bcast, 1)
            pe.matmul(pKV[1][:, 0:RANK], ones[0:1, :], rows[:, D:], start=True, stop=True).then_inc(s_bcast, 1)
            pe.wait_ge(s_abs, 1)
            pe.matmul(pK[:, 0, 0:1], ones[:, :], wsum[:, 0:1], start=True, stop=True).then_inc(s_total, 1)
            for a in range(2):
                for it in range(IT):
                    mm = pe.transpose(pX[a][:, it, 0:96], w_kva[:, a, it * P:(it + 1) * P], ident[0:96, 0:96])
                mm.then_inc(s_aT, 1)
            pe.wait_ge(s_tern, 5)
            for it in range(IT):
                need(pe, s_wT_l, it - 1)
                for a in range(IT):
                    mm = pe.transpose(p_ffn[it % 2][:, a * P:(a + 1) * P], w_ste[:, a, it * P:(it + 1) * P],
                                      ident[:, :])
                mm.then_inc(s_wT, 1)
            pe.wait_ge(s_wT_l, IT)
            pe.wait_ge(s_aT_l, 1)
            pe.wait_ge(s_bcast_out, 2)
            pe.wait_ge(s_order, 1)

            def round_(c, more):
                for s in range(4 * QB):
                    if s < 4:
                        transpose_x(c, s)
                    if s in (4, 5, 7, 9):
                        latent(c, (4, 5, 7, 9).index(s))
                    if s in (6, 8, 10, 11):
                        linear(c, (6, 8, 10, 11).index(s))
                    if s >= 12:
                        transpose_keys(c, s - 12)
                    weights(c, s // 4, s % 4)

            rounds(ENG.PE, round_)


def build_attention(nc, t, keep):
    with ExitStack() as ctx:
        def sb(name, shape, dt=F32):
            return ctx.enter_context(nc.sbuf_tensor(name, shape, dt))

        def ps(name, shape=(P, 512)):
            return ctx.enter_context(nc.psum_tensor(name, list(shape), F32))

        def sem(name):
            return ctx.enter_context(nc.semaphore(name))

        xT, cosT, sinT, Wq, Wp, Wv = (keep[k] for k in ("xT", "cosT", "sinT", "Wq", "Wp", "Wv"))
        acc = [keep["acc0"], sb("acc1", [P, QB, D])]
        q_h = [sb(f"q_h{i}", [P, CW], F32R) for i in range(2)]
        q_l = [sb(f"q_l{i}", [P, CW], F32R) for i in range(2)]
        qp_h = [sb(f"qp_h{i}", [P, CW], F32R) for i in range(2)]
        qp_l = [sb(f"qp_l{i}", [P, CW], F32R) for i in range(2)]
        probs = [sb(f"probs{i}", [P, QB, S]) for i in range(2)]
        pT_h = [sb(f"pT_h{i}", [P, CW], F32R) for i in range(PT_RING)]
        pT_l = [sb(f"pT_l{i}", [P, CW], F32R) for i in range(PT_RING)]
        o_h = sb("o_h", [P, CW], F32R)
        o_l = sb("o_l", [P, CW], F32R)
        rot_cos = sb("rot_cos", [P, CW])
        rot_sin = sb("rot_sin", [P, CW])
        rotated = sb("rotated", [P, CW])
        part_max = [sb(f"part_max{i}", [P, QB, NCH]) for i in range(2)]
        neg_max = [sb(f"neg_max{i}", [P, QB]) for i in range(2)]
        row_sum = [sb(f"row_sum{i}", [P, QB]) for i in range(2)]
        inv_sum = [sb(f"inv_sum{i}", [P, QB]) for i in range(2)]
        ident, ident16, mask = keep["ident"], keep["ident16"], keep["mask"]
        Kn_h, Kn_l, Kp = (keep[k] for k in ("Kn_h", "Kn_l", "Kp"))
        V_h, V_l = (keep[k][:, :].rearrange("p (n c) -> p n c", c=RANK) for k in ("V_h", "V_l"))

        p_score = [ps(f"p_score{i}") for i in range(2)]
        p_tr = [ps(f"p_tr{i}") for i in range(PT_RING)]
        p_out = ps("p_out")
        p_lat = ps("p_lat")
        p_rot = ps("p_rot")
        p_result = p_tr + [p_out]

        chunk_in = sem("chunk_in")
        wq_in = [sem(f"wq_in{i}") for i in range(2)]
        wp_in = sem("wp_in")
        wv_in = [sem(f"wv_in{i}") for i in range(2)]
        result_out = sem("result_out")
        rot_projected = sem("rot_projected")
        lat_projected = sem("lat_projected")
        scored = sem("scored")
        transposed = sem("transposed")
        pv_done = sem("pv_done")
        out_projected = sem("out_projected")
        copied = sem("copied")
        maxed = sem("maxed")
        rot_read = sem("rot_read")
        pT_split = sem("pT_split")
        o_split = sem("o_split")
        q_split = sem("q_split")
        inverted = sem("inverted")
        accumulated = sem("accumulated")
        exped = sem("exped")
        pT_high = sem("pT_high")
        o_high = sem("o_high")
        q_high = sem("q_high")
        qp_high = sem("qp_high")
        rot_added = sem("rot_added")
        qp_ready = sem("qp_ready")

        block = ctx.enter_context(nc.Block())
        result = t["out"].rearrange("(c a p) o -> c p a o", a=QB, p=P)

        @block.sync
        def _(sp):
            def load_q(pos):
                if pos[2] == 0:
                    sp.wait_ge(rot_projected, pairs_before(pos))
                    sp.dma_start(Wp[:, :, :, :].bitcast(F32), t["wp_scr"][pos[1]]).then_inc(wp_in, 16)
                sp.wait_ge(lat_projected, heads_before(pos) - 1)
                sp.dma_start(Wq[pos[2]][:, :, :, :].bitcast(F32), t["wq_scr"][2 * pos[1] + pos[2]]).then_inc(wq_in[pos[2]], 16)

            def load_v(pos):
                sp.wait_ge(out_projected, QB * (heads_before(pos) - 1))
                sp.dma_start(Wv[pos[2]][:, :, :].bitcast(F32), t["wv_scr"][2 * pos[1] + pos[2]]).then_inc(wv_in[pos[2]], 16)

            def load_chunk(j):
                sp.wait_ge(lat_projected, H * j)
                sp.wait_ge(rot_projected, H // 2 * j)
                sp.dma_start(xT[:, :, :, :].bitcast(F32), t["xT_scr"][j]).then_inc(chunk_in, 16)
                sp.wait_ge(rot_read, H // 2 * j)
                sp.dma_start(cosT[:, :], t["cosT"][j]).then_inc(chunk_in, 16)
                sp.dma_start(sinT[:, :], t["sinT"][j]).then_inc(chunk_in, 16)
                if j >= 2:
                    sp.wait_ge(result_out, 16 * (j - 1))
                sp.dma_start(acc[j % 2][:, :, :], t["acc_scr"][j]).then_inc(chunk_in, 16)

            def store_chunk(j):
                sp.wait_ge(accumulated, QB * H * (j + 1))
                sp.dma_start(result[j], acc[j % 2][:, :, :]).then_inc(result_out, 16)

            for j in range(NCH):
                if j >= 1:
                    load_chunk(j)
                    for p in range(2):
                        load_q((j, 0, p))
                        load_v((j, 0, p))
                    store_chunk(j - 1)
                with nc.Fori(1, H // 2, engines=[ENG.SP]) as m:
                    for p in range(2):
                        load_q((j, m, p))
                        load_v((j, m, p))
            store_chunk(NCH - 1)
            sp.wait_ge(result_out, 16 * NCH)

        @block.tensor
        def _(pe):
            def project_rotary(pos):
                need(pe, wp_in, 16 * pairs_before(pos))
                if first_of_chunk(pos):
                    need(pe, chunk_in, 64 * pos[0])
                need(pe, rot_read, pairs_before(pos))
                product(p_rot[:, :], Wp, rot_projected)

            def project_latent(pos):
                g, p = heads_before(pos), pos[2]
                need(pe, wq_in[p], 16 * pairs_before(pos))
                need(pe, q_split, g)
                product(p_lat[:, :], Wq[p], lat_projected)

            def product(out, weights, done):
                for it in range(IT):
                    for k, (w, x) in enumerate(((0, 0), (0, 1), (1, 0))):
                        mm = pe.matmul(out, weights[:, w, it, :], xT[:, x, it, :], start=(it == 0 and k == 0),
                                       stop=(it == IT - 1 and k == 2))
                mm.then_inc(done, 1)

            def scores(pos, u):
                j, p = pos[0], pos[2]
                i, b = u // (j + 1), u % (j + 1)
                width = P * (i + 1) if b == j else CW
                if u == 0:
                    pe.wait_ge(q_split, heads_before(pos) + 1)
                    pe.wait_ge(qp_ready, 2 * heads_before(pos) + 2)
                need(pe, copied, tiles_before(pos) + u - 1)
                rows, keys = slice(i * P, (i + 1) * P), slice(b * CW, b * CW + width)
                out = p_score[u % 2]
                for k, (q, kk) in enumerate(((q_h, Kn_h), (q_h, Kn_l), (q_l, Kn_h), (qp_h, Kp), (qp_l, Kp))):
                    mm = pe.matmul(out[:, 0:width], q[p][:, rows], kk[:, keys], start=(k == 0),
                                   stop=(k == 4 and b < j))
                if b == j:
                    mm = pe.matmul(out[:, width - P:width], ident16[:, :], mask[:, :], start=False, stop=True)
                mm.then_inc(scored, 1)

            def transposes(pos, k):
                n, p = tiles_before(pos), pos[2]
                if k == 0:
                    pe.wait_ge(exped, rows_before(pos) + QB)
                if k >= PT_RING:
                    need(pe, pT_split, n + k - PT_RING + 1)
                else:
                    need(pe, accumulated, QB * (heads_before(pos) - 1) + k + 1)
                for i in range(first_row(pos, k), QB):
                    mm = pe.transpose(p_tr[k % PT_RING][:, i * P:(i + 1) * P], probs[p][:, i, k * P:(k + 1) * P],
                                      ident[:, :])
                mm.then_inc(transposed, 1)

            def values(pos, k):
                if k == 0:
                    need(pe, accumulated, QB * heads_before(pos))
                pe.wait_ge(pT_split, tiles_before(pos) + k + 1)
                cols, r = slice(first_row(pos, k) * P, CW), k % PT_RING
                last = k == tiles_of(pos) - 1
                for a, (v, pt) in enumerate(((V_h, pT_h), (V_h, pT_l), (V_l, pT_h))):
                    mm = pe.matmul(p_out[:, cols], v[:, k, :], pt[r][:, cols], start=(k == 0 and a == 0),
                                   stop=(last and a == 2))
                mm.then_inc(pv_done, 1)

            def project_out(pos, i):
                g, p = heads_before(pos), pos[2]
                if i == 0:
                    pe.wait_ge(o_split, g + 1)
                    need(pe, wv_in[p], 16 * pairs_before(pos))
                out, rows = p_result[i], slice(i * P, (i + 1) * P)
                for k, (o, w) in enumerate(((o_h, 0), (o_h, 1), (o_l, 0))):
                    mm = pe.matmul(out[:, :], o[:, rows], Wv[p][:, w, :], start=(k == 0), stop=(k == 2))
                mm.then_inc(out_projected, 1)

            def step(cur, prev, nxt):
                units = tiles_of(cur) if cur else tiles_of(prev)
                tiles = tiles_of(prev) if prev else 0
                done = 0
                for u in range(units):
                    if cur:
                        scores(cur, u)
                    if u < tiles:
                        transposes(prev, u)
                    if u >= 2 and u - 2 < tiles:
                        values(prev, u - 2)
                        done = u - 1
                    if nxt and nxt[2] == 0 and u == units // 2:
                        project_rotary(nxt)
                for k in range(done, tiles):
                    values(prev, k)
                if nxt:
                    project_latent(nxt)
                if prev:
                    for i in range(QB):
                        project_out(prev, i)

            project_rotary((0, 0, 0))
            project_latent((0, 0, 0))
            walk(nc, ENG.PE, step)

        @block.vector
        def _(dve):
            def copy_scores(pos, u):
                j, p = pos[0], pos[2]
                i, b = u // (j + 1), u % (j + 1)
                width = P * (i + 1) if b == j else CW
                n = tiles_before(pos) + u
                dve.wait_ge(scored, n + 1)
                dve.tensor_scalar(probs[p][:, i, b * CW:b * CW + width], p_score[u % 2][:, 0:width], SCALE, LOWEST,
                                  ALU.mult, ALU.max, accum_out=part_max[p][:, i, b:b + 1]).then_inc(copied, 1)
                if b == j:
                    dve.wait_ge(copied, n + 1)
                    need(dve, exped, rows_before(pos) - QB)
                    dve.tensor_reduce(neg_max[p][:, i:i + 1], part_max[p][:, i, 0:j + 1], AXX, ALU.max,
                                      negate=True).then_inc(maxed, 1)

            def split_tile(pos, k):
                r, cols = k % PT_RING, slice(first_row(pos, k) * P, CW)
                dve.wait_ge(pT_high, tiles_before(pos) + k + 1)
                dve.tensor_tensor(pT_l[r][:, cols], p_tr[r][:, cols], pT_h[r][:, cols].bitcast(F32),
                                  ALU.subtract).then_inc(pT_split, 1)

            def rotate(pos):
                if first_of_chunk(pos):
                    need(dve, chunk_in, 64 * pos[0])
                dve.wait_ge(rot_projected, pairs_before(pos) + 1)
                need(dve, rot_added, pairs_before(pos))
                dve.tensor_tensor(rot_cos[:, :], p_rot[:, :], cosT[:, :], ALU.mult)
                for q in range(P // HALF):
                    to, of = slice(HALF * q, HALF * (q + 1)), slice(HALF * (q ^ 1), HALF * ((q ^ 1) + 1))
                    last = dve.tensor_tensor(rot_sin[to, :], p_rot[of, :], sinT[of, :], ALU.mult)
                last.then_inc(rot_read, 1)

            def split_query(pos):
                p = pos[2]
                dve.wait_ge(q_high, heads_before(pos) + 1)
                dve.tensor_tensor(q_l[p][:, :], p_lat[:, :], q_h[p][:, :].bitcast(F32), ALU.subtract).then_inc(q_split, 1)

            def split_output(pos):
                dve.wait_ge(o_high, heads_before(pos) + 1)
                dve.tensor_tensor(o_l[:, :], p_out[:, :], o_h[:, :].bitcast(F32), ALU.subtract).then_inc(o_split, 1)

            def accumulate(pos):
                g, p = heads_before(pos), pos[2]
                a = acc[pos[0] % 2]
                dve.wait_ge(exped, rows_before(pos) + QB)
                need(dve, accumulated, QB * g)
                dve.reciprocal(inv_sum[p][:, :], row_sum[p][:, :]).then_inc(inverted, 1)
                dve.wait_ge(inverted, g + 1)
                for i in range(QB):
                    dve.wait_ge(out_projected, QB * g + i + 1)
                    dve.scalar_tensor_tensor(out=a[:, i, :], in0=p_result[i][:, :],
                                             scalar=inv_sum[p][:, i:i + 1], in1=a[:, i, :],
                                             op0=ALU.mult, op1=ALU.add).then_inc(accumulated, 1)

            def step(cur, prev, nxt):
                units = tiles_of(cur) if cur else tiles_of(prev)
                tiles = tiles_of(prev) if prev else 0
                for u in range(units):
                    if cur:
                        copy_scores(cur, u)
                    if u < tiles:
                        split_tile(prev, u)
                    if nxt and nxt[2] == 0 and u == units // 2:
                        rotate(nxt)
                if prev:
                    split_output(prev)
                if nxt:
                    split_query(nxt)
                if prev:
                    accumulate(prev)

            rotate((0, 0, 0))
            split_query((0, 0, 0))
            walk(nc, ENG.DVE, step)

        @block.scalar
        def _(act):
            def exp_row(pos, i):
                p, width = pos[2], P * (QB * pos[0] + i + 1)
                act.wait_ge(maxed, rows_before(pos) + i + 1)
                need(act, inverted, heads_before(pos) - 1)
                act.activation(probs[p][:, i, 0:width], probs[p][:, i, 0:width], ACT.Exp,
                               bias=neg_max[p][:, i:i + 1], scale=1.0,
                               accum_out=row_sum[p][:, i:i + 1]).then_inc(exped, 1)

            def high_tile(pos, k):
                r, cols, n = k % PT_RING, slice(first_row(pos, k) * P, CW), tiles_before(pos)
                act.wait_ge(transposed, n + k + 1)
                need(act, pv_done, n + k - PT_RING + 1 if k >= PT_RING else n)
                act.activation(pT_h[r][:, cols], p_tr[r][:, cols], ACT.Copy).then_inc(pT_high, 1)

            def high_output(pos):
                g = heads_before(pos)
                act.wait_ge(pv_done, tiles_before(pos) + tiles_of(pos))
                need(act, out_projected, QB * g)
                act.activation(o_h[:, :], p_out[:, :], ACT.Copy).then_inc(o_high, 1)

            def high_query(pos):
                act.wait_ge(lat_projected, heads_before(pos) + 1)
                free_query(pos)
                act.activation(q_h[pos[2]][:, :], p_lat[:, :], ACT.Copy).then_inc(q_high, 1)

            def high_rotary(pos):
                p = pos[2]
                act.wait_ge(rot_added, pairs_before(pos) + 1)
                free_query(pos)
                for half in (slice(0, ROPE), slice(ROPE, P)):
                    last = act.activation(qp_h[p][half, :], rotated[ROPE * p:ROPE * (p + 1), :], ACT.Copy)
                last.then_inc(qp_high, 1)

            def free_query(pos):
                j, m, p = pos
                if first_of_chunk(pos):
                    need(act, scored, tiles_before((j - 1, H // 2 - 1, 1)) if j else 0)
                else:
                    need(act, scored, tiles_before((j, m, 0)) if p else tiles_before((j, m - 1, 1)))

            def step(cur, prev, nxt):
                units = tiles_of(cur) if cur else tiles_of(prev)
                tiles = tiles_of(prev) if prev else 0
                for u in range(units):
                    if u < tiles:
                        high_tile(prev, u)
                    if cur and (u + 1) % (cur[0] + 1) == 0:
                        exp_row(cur, u // (cur[0] + 1))
                    if cur and cur[2] == 0 and u == 1:
                        high_rotary(nxt)
                if prev:
                    high_output(prev)
                if nxt and nxt[2] == 0:
                    high_rotary(nxt)
                if nxt:
                    high_query(nxt)

            high_rotary((0, 0, 0))
            high_query((0, 0, 0))
            walk(nc, ENG.Activation, step)

        @block.gpsimd
        def _(pool):
            def add_rotary(pos):
                pool.wait_ge(rot_read, pairs_before(pos) + 1)
                need(pool, qp_ready, 2 * heads_before(pos))
                pool.tensor_tensor(rotated[:, :], rot_cos[:, :], rot_sin[:, :], ALU.add).then_inc(rot_added, 1)

            def low_rotary(pos):
                p = pos[2]
                own = slice(ROPE * p, ROPE * (p + 1))
                pool.wait_ge(qp_high, heads_before(pos) + 1)
                if p:
                    pool.wait_ge(qp_ready, 2 * heads_before(pos))
                else:
                    pool.wait_ge(rot_added, pairs_before(pos) + 1)
                pool.tensor_tensor(qp_l[p][0:ROPE, :], rotated[own, :], qp_h[p][own, :].bitcast(F32),
                                   ALU.subtract).then_inc(qp_ready, 1)
                pool.wait_ge(qp_ready, 2 * heads_before(pos) + 1)
                pool.tensor_tensor(qp_l[p][ROPE:P, :], rotated[own, :], qp_h[p][own, :].bitcast(F32),
                                   ALU.subtract).then_inc(qp_ready, 1)

            def step(cur, prev, nxt):
                if nxt and nxt[2] == 0:
                    add_rotary(nxt)
                if nxt:
                    low_rotary(nxt)

            add_rotary((0, 0, 0))
            low_rotary((0, 0, 0))
            walk(nc, ENG.Pool, step)


def build(nc, t):
    with ExitStack() as ctx:
        def sb(name, shape, dt=F32):
            return ctx.enter_context(nc.sbuf_tensor(name, shape, dt))

        keep = {
            "ident": sb("ident", [P, P]),
            "ident16": sb("ident16", [P, P], BF16),
            "mask": sb("mask_bf16", [P, P], BF16),
            "mask_f32": sb("mask_f32", [P, P]),
            "order_f32": sb("order_f32", [P, ROPE]),
            "Kn_h": sb("Kn_h", [P, S], F32R),
            "Kn_l": sb("Kn_l", [P, S], F32R),
            "Kp": sb("Kp", [P, S], F32R),
            "V_h": sb("V_h", [P, NT * RANK], F32R),
            "V_l": sb("V_l", [P, NT * RANK], F32R),
            "xT": sb("xT", [P, 2, IT, CW], F32R),
            "acc0": sb("acc0", [P, QB, D]),
            "cosT": sb("cosT_sb", [P, CW]),
            "sinT": sb("sinT_sb", [P, CW]),
            "Wq": [sb(f"Wq{i}", [P, 2, IT, P], F32R) for i in range(2)],
            "Wp": sb("Wp", [P, 2, IT, P], F32R),
            "Wv": [sb(f"Wv{i}", [P, 2, D], F32R) for i in range(2)],
        }
        build_prepare(nc, t, keep)
        build_attention(nc, t, keep)


def constants():
    freqs = 1.0 / 10000.0 ** (np.arange(0, ROPE, 2, dtype=np.float32) / ROPE)
    ang = np.outer(np.arange(S, dtype=np.float32), freqs)
    cos, sin = np.cos(ang), np.sin(ang)
    by_token = lambda a: np.ascontiguousarray(np.concatenate([a, a], 1).reshape(NT, P, ROPE).transpose(1, 0, 2))
    by_chunk = lambda a: np.ascontiguousarray(a.T.reshape(P, NCH, CW).transpose(1, 0, 2))
    order = np.zeros((2, ROPE, ROPE), np.float32)
    for x in range(2):
        for f in range(HALF):
            order[:, 2 * f + x, HALF * x + f] = 1.0
    return {
        "ident": np.eye(P, dtype=np.float32),
        "mask": np.where(np.tril(np.ones((P, P), bool)), 0.0, MASKED).astype(np.float32),
        "order": order.reshape(P, ROPE),
        "cosN": by_token(cos),
        "sinN": by_token(sin),
        "cosT": by_chunk(np.concatenate([cos] * 4, 1)),
        "sinT": by_chunk(np.concatenate([sin, -sin, sin, -sin], 1)),
    }


_INS = {"x": "L0_attn_x", "wq": "L0_attn_wq", "wkv_a": "L0_attn_wkv_a", "wkv_b": "L0_attn_wkv_b",
        "wo": "L0_attn_wo", "kv_norm_w": "L0_attn_kv_norm_w", "w_ffn": "L0_ffn_weight", "b_ffn": "L0_ffn_bias"}


def kernel(**inputs):
    import concourse.bacc as bacc
    from concourse.bass_utils import run_bass_kernel_spmd

    arrays = {name: np.ascontiguousarray(inputs[key]) for name, key in _INS.items()}
    arrays["x"] = arrays["x"].reshape(S, D)
    arrays.update(constants())
    nc = bacc.Bacc("TRN2", target_bir_lowering=False, num_devices=1)
    t, feeds = {}, {}
    for name, a in arrays.items():
        t[name] = nc.dram_tensor(f"in_{name}", a.shape, F32, kind="ExternalInput").ap()
        feeds[f"in_{name}"] = a
    t["out"] = nc.dram_tensor("out_0", (S, D), F32, kind="ExternalOutput").ap()
    for name, shape, dt in (("xT_scr", (NCH, P, 2, IT, CW), F32), ("acc_scr", (NCH, P, QB, D), F32),
                            ("wq_scr", (H, P, 2, IT, P), F32), ("wp_scr", (H // 2, P, 2, IT, P), F32), ("wv_scr", (H, P, 2, D), F32)):
        t[name] = nc.dram_tensor(name, shape, dt, kind="Internal").ap()
    build(nc, t)
    r = run_bass_kernel_spmd(nc, [feeds], core_ids=[0])
    return r.results[0]["out_0"].reshape(1, S, D)
```

```python
from contextlib import ExitStack

import numpy as np

import concourse.bass as bass
from concourse import mybir

ALU = mybir.AluOpType
ACT = mybir.ActivationFunctionType
AXX = mybir.AxisListType.X
F32 = mybir.dt.float32
F32R = mybir.dt.float32r
BF16 = mybir.dt.bfloat16
ENG = mybir.EngineType

P = 128
S = 2048
D = 512
H = 16
NOPE = 128
ROPE = 64
HALF = ROPE // 2
RANK = 128
VDIM = 128
QK = NOPE + ROPE
IT = D // P
CW = 512
NCH = S // CW
QB = CW // P
NT = S // P
SCALE = float(QK) ** -0.5
MASKED = -1.0e30
LN_EPS = 1e-5
RMS_EPS = 1e-6
FFN_EPS = 1e-10
LINEAR_SLOTS = {5: (0,), 6: (1,), 7: (2, 3)}
LOWEST = -3.0e38
PT_RING = 3


def need(eng, sem, value):
    if isinstance(value, int) and value <= 0:
        return
    eng.wait_ge(sem, value)


def heads_before(pos):
    j, m, p = pos
    return H * j + 2 * m + p


def tiles_before(pos):
    j, m, p = pos
    return QB * H * (j * (j + 1) // 2) + QB * (j + 1) * (2 * m + p)


def rows_before(pos):
    return QB * heads_before(pos)


def pairs_before(pos):
    j, m, p = pos
    return (H // 2) * j + m


def tiles_of(pos):
    return QB * (pos[0] + 1)


def first_of_chunk(pos):
    return isinstance(pos[1], int) and pos[1:] == (0, 0)


def first_row(pos, k):
    return max(0, k - QB * pos[0])


def rotary_unit(nxt, units):
    if nxt[2]:
        return None
    return units * 3 // 4 if first_of_chunk(nxt) else units // 2 - (1 if units == QB else 0)


def walk(nc, engine, step):
    def two_steps(j, m):
        step((j, m, 1), (j, m, 0), (j, m + 1, 0))
        step((j, m + 1, 0), (j, m, 1), (j, m + 1, 1))

    for j in range(NCH):
        step((j, 0, 0), (j - 1, H // 2 - 1, 1) if j else None, (j, 0, 1))
        if j == 0:
            two_steps(0, 0)
        with nc.Fori(0 if j else 1, H // 2 - 1, engines=[engine]) as m:
            two_steps(j, m)
        step((j, H // 2 - 1, 1), (j, H // 2 - 1, 0), (j + 1, 0, 0) if j + 1 < NCH else None)
    step(None, (NCH - 1, H // 2 - 1, 1), None)


def build_prepare(nc, t, keep, stored):
    with ExitStack() as ctx:
        def sb(name, shape, dt=F32):
            return ctx.enter_context(nc.sbuf_tensor(name, shape, dt))

        def ps(name, shape):
            return ctx.enter_context(nc.psum_tensor(name, shape, F32))

        def sem(name):
            return ctx.enter_context(nc.semaphore(name))

        ident, xT, residual = keep["ident"], keep["xT"], keep["acc0"]
        Wq, Wp, Wv = keep["Wq"], keep["Wp"], keep["Wv"]
        w_ffn = sb("w_ffn", [P, IT, D])
        ffnT_h = sb("ffnT_h", [P, IT, D], F32R)
        ffnT_l = sb("ffnT_l", [P, IT, D], F32R)
        w_kva = sb("w_kva", [96, 2, D])
        kvaT_h = sb("kvaT_h", [P, IT, 192], F32R)
        kvaT_l = sb("kvaT_l", [P, IT, 192], F32R)
        rows = sb("rows", [1, D + RANK])
        ones = sb("ones", [P, P])
        bias_all = sb("bias_all", [P, D])
        norm_all = sb("norm_all", [P, RANK])
        wsum = sb("wsum", [P, 8])
        minus_half = sb("minus_half", [P, QB])
        x_in = sb("x_in", [P, QB, D])
        xhat = sb("xhat", [P, QB, D])
        xb = sb("xb", [P, QB, D])
        stats = sb("stats", [P, QB, 6])
        moments = sb("moments", [P, QB, 2])
        var_eps = sb("var_eps", [P, QB])
        rstd = sb("rstd", [P, QB])
        squares = sb("squares", [P, RANK])
        sumsq = sb("sumsq", [P, QB])
        ms = sb("ms", [P, QB])
        rrms = sb("rrms", [P, QB])
        lat = sb("lat", [P, QB, RANK])
        by_cos = sb("by_cos", [P, QB, ROPE])
        by_sin = sb("by_sin", [P, QB, ROPE])
        roped = sb("roped", [P, QB, ROPE])
        kpe = sb("kpe", [P, QB, 2, ROPE], F32R)
        cosN = sb("cosN_sb", [P, NT * ROPE])
        sinN = sb("sinN_sb", [P, NT * ROPE])
        wqn = [sb(f"wqn{i}", [P, D]) for i in range(2)]
        wqn_h = [sb(f"wqn_h{i}", [P, D], F32R) for i in range(2)]
        wqn_l = [sb(f"wqn_l{i}", [P, D], F32R) for i in range(2)]
        wqp = sb("wqp", [P, D])
        wqp_h = sb("wqp_h", [P, D], F32R)
        wqp_l = sb("wqp_l", [P, D], F32R)
        order = sb("order", [P, ROPE], F32R)
        wkb = [sb(f"wkb{i}", [P, 2, RANK]) for i in range(2)]
        wkb_h = [sb(f"wkb_h{i}", [P, 2, RANK], F32R) for i in range(2)]
        wkb_l = [sb(f"wkb_l{i}", [P, 2, RANK], F32R) for i in range(2)]
        wo = [sb(f"wo{i}", [P, IT, VDIM]) for i in range(2)]
        woT_h = sb("woT_h", [P, D], F32R)
        woT_l = sb("woT_l", [P, D], F32R)
        w_flat = w_ffn[:, :, :].rearrange("p a i -> p (a i)")
        w_pos = residual[:, :, :].rearrange("p a i -> p (a i)")
        w_neg = xb[:, :, :].rearrange("p a i -> p (a i)")
        w_ste = residual

        pX = [ps(f"pX{i}", [P, IT, P]) for i in range(2)]
        pKV = [ps(f"pKV{i}", [P, 512]) for i in range(2)]
        pF = [ps(f"pF{i}", [P, D]) for i in range(2)]
        pW = [ps(f"pW{i}", [P, 512]) for i in range(2)]
        pQ = pW[0][:, :].rearrange("p (a c) -> p a c", a=IT)
        pP = pW[1][:, :].rearrange("p (k a c) -> p k a c", k=2, a=IT)

        s_const = sem("s_const")
        s_tables = sem("s_tables")
        s_w = sem("s_w")
        s_ones = sem("s_ones")
        s_bcast = sem("s_bcast")
        s_bcast_out = sem("s_bcast_out")
        s_abs = sem("s_abs")
        s_total = sem("s_total")
        s_thr = sem("s_thr")
        s_tern = sem("s_tern")
        s_wT = sem("s_wT")
        s_wT_h = sem("s_wT_h")
        s_wT_l = sem("s_wT_l")
        s_aT = sem("s_aT")
        s_aT_h = sem("s_aT_h")
        s_aT_l = sem("s_aT_l")
        s_x = sem("s_x")
        s_stats = sem("s_stats")
        s_moments = sem("s_moments")
        s_var = sem("s_var")
        s_rstd = sem("s_rstd")
        s_xhat = sem("s_xhat")
        s_xb = sem("s_xb")
        s_xT = sem("s_xT")
        s_xT_h = sem("s_xT_h")
        s_xT_l = sem("s_xT_l")
        s_kv = sem("s_kv")
        s_sumsq = sem("s_sumsq")
        s_ms = sem("s_ms")
        s_rrms = sem("s_rrms")
        s_rot = sem("s_rot")
        s_lat = sem("s_lat")
        s_roped = sem("s_roped")
        s_vh = sem("s_vh")
        s_kpe_h = sem("s_kpe_h")
        s_kpe_l = sem("s_kpe_l")
        s_ffn = sem("s_ffn")
        s_acc = sem("s_acc")
        s_kT = sem("s_kT")
        s_kT_h = sem("s_kT_h")
        s_kT_l = sem("s_kT_l")
        s_load = [sem(f"s_load{i}") for i in range(2)]
        s_order = sem("s_order")
        s_high = sem("s_high")
        s_low = sem("s_low")
        s_woT = sem("s_woT")
        s_woT_h = sem("s_woT_h")
        s_woT_l = sem("s_woT_l")
        s_xT_out, s_acc_out, s_wq_out, s_wv_out, s_wp_out = (stored[k] for k in ("xT", "acc", "wq", "wv", "wp"))
        s_pe = sem("s_pe")
        s_pe_h = sem("s_pe_h")
        s_pe_l = sem("s_pe_l")
        s_q = sem("s_q")
        s_q_h = sem("s_q_h")
        s_q_l = sem("s_q_l")
        s_v = sem("s_v")
        s_v_h = sem("s_v_h")
        s_v_l = sem("s_v_l")

        block = ctx.enter_context(nc.Block())
        wq_heads = t["wq"].rearrange("(h r) i -> h r i", h=H)
        wkb_heads = t["wkv_b"].rearrange("(h two d) c -> h d two c", h=H, two=2)
        wo_heads = t["wo"].rearrange("(a p) (h d) -> h p a d", p=P, h=H)
        x_chunks = t["x"].rearrange("(c a p) i -> c p a i", a=QB, p=P)

        def rounds(engine, round_):
            round_(0, True, True)
            with nc.Fori(1, NCH - 1, engines=[engine]) as c:
                round_(c, False, True)
            round_(NCH - 1, False, False)

        def at(tensor, c, b, n=1):
            return tensor[:, bass.ds(c * (-n * QB) + n * (QB * (NCH - 1) + b), n)]

        @block.sync
        def _(sp):
            def load_head(c, k):
                h, i = c * -QB + (H - 1 - k), k % 2
                sp.dma_start(wqp[ROPE * i:ROPE * (i + 1), :], wq_heads[h][NOPE:QK, :]).then_inc(s_load[i], 16)
                sp.dma_start(wkb[i][:, :, :], wkb_heads[h]).then_inc(s_load[i], 16)
                sp.dma_start(wqn[i][:, :], wq_heads[h][0:NOPE, :]).then_inc(s_load[i], 16)
                sp.dma_start(wo[i][:, :, :], wo_heads[h]).then_inc(s_load[i], 16)

            sp.dma_start(ident[:, :], t["ident"]).then_inc(s_const, 16)
            sp.dma_start(w_kva[:, :, :], t["wkv_a"].rearrange("(a p) i -> p a i", p=96)).then_inc(s_const, 16)
            sp.dma_start(x_in[:, :, :], x_chunks[NCH - 1]).then_inc(s_x, 16)
            load_head(0, 0)
            load_head(0, 1)
            sp.dma_start(cosN[:, :], t["cosN"].rearrange("p n c -> p (n c)")).then_inc(s_tables, 16)
            sp.dma_start(sinN[:, :], t["sinN"].rearrange("p n c -> p (n c)")).then_inc(s_tables, 16)
            sp.dma_start(keep["cosT"][:, :], t["cosT"][0]).then_inc(s_tables, 16)
            sp.dma_start(keep["sinT"][:, :], t["sinT"][0]).then_inc(s_tables, 16)

            def round_(c, first, more):
                d = c * -1 + (NCH - 1)
                for k in range(QB):
                    n, h = QB * c + k, c * -QB + (H - 1 - k)
                    if more or k < 2:
                        sp.wait_ge(s_woT, n + 1)
                        sp.wait_ge(s_high, 3 * n + 3)
                        sp.wait_ge(s_low, 3 * n + 3)
                        load_head(c, k + 2)
                    if k == 0 and more:
                        sp.wait_ge(s_xhat, QB * (c + 1))
                        sp.wait_ge(s_xb, QB * (c + 1))
                        sp.dma_start(x_in[:, :, :], x_chunks[d - 1]).then_inc(s_x, 16)
                    if k % 2:
                        sp.wait_ge(s_pe_h, n + 1)
                        sp.wait_ge(s_pe_l, n + 1)
                        sp.dma_start(t["wp_scr"][c * -2 + (H // 2 - 1 - k // 2)],
                                     Wp[:, :, :, :].bitcast(F32)).then_inc(s_wp_out, 16)
                    sp.wait_ge(s_q_l, n + 1)
                    sp.dma_start(t["wq_scr"][h], Wq[1 - k % 2][:, :, :, :].bitcast(F32)).then_inc(s_wq_out[k % 2], 16)
                    sp.wait_ge(s_v_l, n + 1)
                    sp.dma_start(t["wv_scr"][h], Wv[1 - k % 2][:, :, :].bitcast(F32)).then_inc(s_wv_out[k % 2], 16)
                    if k == 1 and more:
                        sp.wait_ge(s_xT_l, QB * (c + 1))
                        sp.dma_start(t["xT_scr"][d], xT[:, :, :, :].bitcast(F32)).then_inc(s_xT_out, 16)
                    if k == 2 and more:
                        sp.wait_ge(s_acc, QB * (c + 1))
                        sp.dma_start(t["acc_scr"][d], residual[:, :, :]).then_inc(s_acc_out, 16)

            rounds(ENG.SP, round_)

        @block.gpsimd
        def _(pool):
            def low_parts(c, k):
                n, i = QB * c + k, k % 2
                half = slice(ROPE * i, ROPE * (i + 1))
                pool.wait_ge(s_high, 3 * n + 1)
                pool.tensor_tensor(wkb_l[i][:, :, :], wkb[i][:, :, :], wkb_h[i][:, :, :].bitcast(F32),
                                   ALU.subtract).then_inc(s_low, 1)
                pool.wait_ge(s_high, 3 * n + 2)
                pool.wait_ge(s_low, 3 * n + 1)
                pool.tensor_tensor(wqp_l[half, :], wqp[half, :], wqp_h[half, :].bitcast(F32),
                                   ALU.subtract).then_inc(s_low, 1)
                pool.wait_ge(s_high, 3 * n + 3)
                pool.wait_ge(s_low, 3 * n + 2)
                pool.tensor_tensor(wqn_l[i][:, :], wqn[i][:, :], wqn_h[i][:, :].bitcast(F32),
                                   ALU.subtract).then_inc(s_low, 1)

            def norm(c):
                need(pool, s_var, c + 1)
                pool.tensor_tensor(rstd[:, :], var_eps[:, :], minus_half[:, :], ALU.pow).then_inc(s_rstd, 1)

            def add_bias(c):
                need(pool, s_acc, QB * c)
                pool.wait_ge(s_x, 16 * (c + 1))
                for b in range(QB):
                    pool.tensor_tensor(xb[:, b, :], x_in[:, b, :], bias_all[:, :], ALU.add).then_inc(s_xb, 1)

            def rotary_key(c, b):
                n = QB * c + b
                pool.wait_ge(s_ms, n + 1)
                pool.tensor_tensor(rrms[:, b:b + 1], ms[:, b:b + 1], minus_half[:, b:b + 1],
                                   ALU.pow).then_inc(s_rrms, 1)
                pool.wait_ge(s_rot, n + 1)
                need(pool, s_kpe_h, QB * c)
                pool.tensor_tensor(roped[:, b, 0:HALF], by_cos[:, b, 0:HALF], by_sin[:, b, HALF:], ALU.subtract)
                pool.tensor_tensor(roped[:, b, HALF:], by_cos[:, b, HALF:], by_sin[:, b, 0:HALF],
                                   ALU.add).then_inc(s_roped, 1)

            def low_keys(c, b):
                n = QB * c + b
                pool.wait_ge(s_kpe_h, n + 1)
                pool.tensor_tensor(kpe[:, b, 1, :], roped[:, b, :], kpe[:, b, 0, :].bitcast(F32),
                                   ALU.subtract).then_inc(s_kpe_l, 1)
                pool.wait_ge(s_vh, n + 1)
                pool.tensor_tensor(at(keep["V_l"], c, b, RANK), lat[:, b, :], at(keep["V_h"], c, b, RANK).bitcast(F32),
                                   ALU.subtract)

            pool.memset(minus_half[:, :], -0.5).then_inc(s_ones, 1)
            pool.wait_ge(s_ones, 2)
            low_parts(0, 0)
            norm(0)

            def round_(c, first, more):
                for s in range(4 * QB):
                    if s == 4 and first:
                        pool.wait_ge(s_bcast_out, 2)
                        pool.wait_ge(s_tern, 3)
                        add_bias(0)
                    if s in (4, 5, 7, 9):
                        rotary_key(c, (4, 5, 7, 9).index(s))
                    if s in (6, 8, 10, 11):
                        low_keys(c, (6, 8, 10, 11).index(s))
                    if s == 11 and more:
                        norm(c + 1)
                    if s == 12 and more:
                        add_bias(c + 1)
                    if s % 4 == 2 and (more or s < 12):
                        low_parts(c, s // 4 + 1)

            rounds(ENG.Pool, round_)

        @block.scalar
        def _(act):
            def high_parts(c, k):
                n, i = QB * c + k, k % 2
                half = slice(ROPE * i, ROPE * (i + 1))
                act.wait_ge(s_load[i], 64 * (2 * c + k // 2 + 1))
                need(act, s_v, n - 1)
                act.activation(wkb_h[i][:, :, :], wkb[i][:, :, :], ACT.Copy).then_inc(s_high, 1)
                act.activation(wqp_h[half, :], wqp[half, :], ACT.Copy).then_inc(s_high, 1)
                act.activation(wqn_h[i][:, :], wqn[i][:, :], ACT.Copy).then_inc(s_high, 1)

            def weights(c, k, part):
                n, i = QB * c + k, k % 2
                if part == 0:
                    act.wait_ge(s_woT, n + 1)
                    need(act, s_v, n)
                    act.activation(woT_h[:, :], pW[0][:, :], ACT.Copy).then_inc(s_woT_h, 1)
                elif part == 1:
                    act.wait_ge(s_pe, n + 1)
                    if i == 0:
                        need(act, s_wp_out, 16 * (2 * c + k // 2))
                    act.activation(Wp[:, 0, :, ROPE * (1 - i):ROPE * (2 - i)], pP[:, 0, :, :],
                                   ACT.Copy).then_inc(s_pe_h, 1)
                elif part == 2:
                    act.wait_ge(s_q, n + 1)
                    need(act, s_wq_out[i], 16 * (2 * c + k // 2))
                    act.activation(Wq[1 - i][:, 0, :, :], pQ, ACT.Copy).then_inc(s_q_h, 1)
                else:
                    act.wait_ge(s_v, n + 1)
                    need(act, s_wv_out[i], 16 * (2 * c + k // 2))
                    act.activation(Wv[1 - i][:, 0, :], pW[1][:, :], ACT.Copy).then_inc(s_v_h, 1)

            def x_high(c, b):
                if b == 0:
                    need(act, s_xT_out, 16 * c)
                act.wait_ge(s_xT, QB * c + b + 1)
                act.activation(xT[:, 0, :, b * P:(b + 1) * P], pX[b % 2][:, :, :], ACT.Copy).then_inc(s_xT_h, 1)

            def square(c, b):
                n = QB * c + b
                act.wait_ge(s_kv, n + 1)
                need(act, s_sumsq, n)
                act.activation(squares[:, :], pKV[b % 2][:, 0:RANK], ACT.Square,
                               accum_out=sumsq[:, b:b + 1]).then_inc(s_sumsq, 1)

            def high_keys(c, b):
                n = QB * c + b
                act.wait_ge(s_roped, n + 1)
                need(act, s_kT, QB * c)
                act.activation(kpe[:, b, 0, :], roped[:, b, :], ACT.Copy).then_inc(s_kpe_h, 1)
                act.wait_ge(s_lat, n + 1)
                act.activation(at(keep["V_h"], c, b, RANK), lat[:, b, :], ACT.Copy).then_inc(s_vh, 1)

            def high_keys_transposed(c, b):
                act.wait_ge(s_kT, QB * c + b + 1)
                keys = pF[1 - b % 2]
                act.activation(at(keep["Kn_h"], c, b, P), keys[:, 0:P], ACT.Copy)
                act.activation(at(keep["Kp"], c, b, P), keys[:, P:2 * P], ACT.Copy).then_inc(s_kT_h, 1)

            act.dma_start(rows[:, 0:D], t["b_ffn"].rearrange("(a n) -> a n", a=1)).then_inc(s_const, 16)
            act.dma_start(rows[:, D:], t["kv_norm_w"].rearrange("(a n) -> a n", a=1)).then_inc(s_const, 16)
            act.dma_start(keep["order_f32"][:, :], t["order"]).then_inc(s_const, 16)
            act.dma_start(keep["mask_f32"][:, :], t["mask"]).then_inc(s_const, 16)
            act.dma_start(w_ffn[:, :, :], t["w_ffn"].rearrange("(a p) i -> p a i", p=P)).then_inc(s_w, 16)
            act.wait_ge(s_const, 16 * 6)
            act.activation(keep["mask"][:, :], keep["mask_f32"][:, :], ACT.Copy)
            act.activation(keep["ident16"][:, :], ident[:, :], ACT.Copy)
            act.activation(order[:, :], keep["order_f32"][:, :], ACT.Copy).then_inc(s_order, 1)
            act.wait_ge(s_aT, 1)
            act.activation(kvaT_h[:, :, 0:96], pX[0][:, :, 0:96], ACT.Copy).then_inc(s_aT_h, 1)
            act.wait_ge(s_aT, 2)
            act.activation(kvaT_h[:, :, 96:128], pX[1][:, :, 0:32], ACT.Copy).then_inc(s_aT_h, 1)
            for x in range(2):
                act.activation(kvaT_h[:, :, 128 + HALF * x:128 + HALF * (x + 1)], pX[1][:, :, 32 + x:96:2],
                               ACT.Copy).then_inc(s_aT_h, 1)
            high_parts(0, 0)
            act.wait_ge(s_w, 16)
            act.activation(w_pos, w_flat, ACT.Abs, accum_out=wsum[:, 0:1]).then_inc(s_abs, 1)

            def high_linear(it):
                act.wait_ge(s_wT, it + 1)
                act.activation(ffnT_h[:, it, :], pF[it % 2][:, :], ACT.Copy).then_inc(s_wT_h, 1)

            def round_(c, first, more):
                for s in range(4 * QB):
                    if s < 4:
                        x_high(c, s)
                    if s in (4, 5, 7, 9):
                        square(c, (4, 5, 7, 9).index(s))
                    if first and s in LINEAR_SLOTS:
                        for it in LINEAR_SLOTS[s]:
                            high_linear(it)
                    if s in (6, 8, 10, 11):
                        high_keys(c, (6, 8, 10, 11).index(s))
                    if s >= 12:
                        high_keys_transposed(c, s - 12)
                    weights(c, s // 4, s % 4)
                    if s % 4 == 1 and (more or s < 12):
                        high_parts(c, s // 4 + 1)

            rounds(ENG.Activation, round_)

        @block.vector
        def _(dve):
            def block_stats(c, b):
                if b == 0:
                    dve.wait_ge(s_x, 16 * (c + 1))
                dve.bn_stats(stats[:, b, :], x_in[:, b, :]).then_inc(s_stats, 4)

            def moments_of_x(c):
                dve.wait_ge(s_ones, 2)
                dve.wait_ge(s_stats, 16 * (c + 1))
                for b in range(QB):
                    dve.bn_aggr(moments[:, b, :], stats[:, b, :]).then_inc(s_moments, 1)
                dve.wait_ge(s_moments, QB * (c + 1))
                dve.tensor_scalar(var_eps[:, :], moments[:, :, 1], LN_EPS, None, ALU.add).then_inc(s_var, 1)

            def scale_x(c, b):
                if b == 0:
                    dve.wait_ge(s_rstd, c + 1)
                    need(dve, s_xT, QB * c)
                dve.tensor_scalar(xhat[:, b, :], x_in[:, b, :], moments[:, b, 0:1], rstd[:, b:b + 1],
                                  ALU.subtract, ALU.mult).then_inc(s_xhat, 1)

            def x_low(c, b):
                cols = slice(b * P, (b + 1) * P)
                dve.wait_ge(s_xT_h, QB * c + b + 1)
                dve.tensor_tensor(xT[:, 1, :, cols], pX[b % 2][:, :, :], xT[:, 0, :, cols].bitcast(F32),
                                  ALU.subtract).then_inc(s_xT_l, 1)

            def linear(c, b):
                dve.wait_ge(s_ffn, QB * c + b + 1)
                dve.wait_ge(s_xb, QB * c + b + 1)
                if b == 0:
                    need(dve, s_acc_out, 16 * c)
                dve.tensor_tensor(residual[:, b, :], pF[b % 2][:, :], xb[:, b, :], ALU.add).then_inc(s_acc, 1)

            def rotary_key(c, b):
                n = QB * c + b
                rotary = pKV[b % 2][:, RANK:RANK + ROPE]
                dve.wait_ge(s_sumsq, n + 1)
                need(dve, s_roped, QB * c)
                dve.tensor_tensor(by_cos[:, b, :], rotary, at(cosN, c, b, ROPE), ALU.mult)
                dve.tensor_tensor(by_sin[:, b, :], rotary, at(sinN, c, b, ROPE), ALU.mult).then_inc(s_rot, 1)
                need(dve, s_rrms, QB * c)
                dve.tensor_scalar(ms[:, b:b + 1], sumsq[:, b:b + 1], 1.0 / RANK, RMS_EPS,
                                  ALU.mult, ALU.add).then_inc(s_ms, 1)

            def latent_row(c, b):
                dve.wait_ge(s_rrms, QB * c + b + 1)
                need(dve, s_kT, QB * c)
                dve.scalar_tensor_tensor(out=lat[:, b, :], in0=pKV[b % 2][:, 0:RANK], scalar=rrms[:, b:b + 1],
                                         in1=norm_all[:, :], op0=ALU.mult, op1=ALU.mult).then_inc(s_lat, 1)

            def low_keys_transposed(c, b):
                dve.wait_ge(s_kT_h, QB * c + b + 1)
                dve.tensor_tensor(at(keep["Kn_l"], c, b, P), pF[1 - b % 2][:, 0:P], at(keep["Kn_h"], c, b, P).bitcast(F32),
                                  ALU.subtract).then_inc(s_kT_l, 1)

            def weights(c, k, part):
                n, i = QB * c + k, k % 2
                if part == 0:
                    dve.wait_ge(s_woT_h, n + 1)
                    dve.tensor_tensor(woT_l[:, :], pW[0][:, :], woT_h[:, :].bitcast(F32),
                                      ALU.subtract).then_inc(s_woT_l, 1)
                elif part == 1:
                    dve.wait_ge(s_pe_h, n + 1)
                    dve.tensor_copy(Wp[:, 1, :, ROPE * (1 - i):ROPE * (2 - i)], pP[:, 1, :, :]).then_inc(s_pe_l, 1)
                elif part == 2:
                    dve.wait_ge(s_q_h, n + 1)
                    dve.tensor_tensor(Wq[1 - i][:, 1, :, :], pQ, Wq[1 - i][:, 0, :, :].bitcast(F32),
                                      ALU.subtract).then_inc(s_q_l, 1)
                else:
                    dve.wait_ge(s_v_h, n + 1)
                    dve.tensor_tensor(Wv[1 - i][:, 1, :], pW[1][:, :], Wv[1 - i][:, 0, :].bitcast(F32),
                                      ALU.subtract).then_inc(s_v_l, 1)

            dve.memset(ones[:, :], 1.0).then_inc(s_ones, 1)
            dve.wait_ge(s_bcast, 2)
            dve.tensor_copy(bias_all[:, :], pKV[0][:, :]).then_inc(s_bcast_out, 1)
            dve.tensor_copy(norm_all[:, :], pKV[1][:, 0:RANK]).then_inc(s_bcast_out, 1)
            for b in range(QB):
                block_stats(0, b)
            moments_of_x(0)
            dve.wait_ge(s_aT_h, 4)
            dve.tensor_tensor(kvaT_l[:, :, 0:96], pX[0][:, :, 0:96], kvaT_h[:, :, 0:96].bitcast(F32), ALU.subtract)
            dve.tensor_tensor(kvaT_l[:, :, 96:128], pX[1][:, :, 0:32], kvaT_h[:, :, 96:128].bitcast(F32),
                              ALU.subtract)
            for x in range(2):
                cols = slice(128 + HALF * x, 128 + HALF * (x + 1))
                kva_low = dve.tensor_tensor(kvaT_l[:, :, cols], pX[1][:, :, 32 + x:96:2],
                                            kvaT_h[:, :, cols].bitcast(F32), ALU.subtract)
            kva_low.then_inc(s_aT_l, 1)
            for b in range(QB):
                scale_x(0, b)

            def quantise(s):
                if s == 0:
                    dve.wait_ge(s_total, 1)
                    dve.tensor_scalar(wsum[:, 1:2], pF[1][:, 0:1], 1.0 / (D * D), None, ALU.mult).then_inc(s_thr, 1)
                    dve.tensor_scalar(wsum[:, 3:4], pF[1][:, 0:1], -1.0 / (D * D), None, ALU.mult).then_inc(s_thr, 1)
                    dve.wait_ge(s_thr, 2)
                    dve.tensor_scalar(wsum[:, 2:3], wsum[:, 1:2], FFN_EPS, 0.5, ALU.add, ALU.mult).then_inc(s_thr, 1)
                    dve.tensor_scalar(wsum[:, 4:5], wsum[:, 1:2], FFN_EPS, -0.5, ALU.add, ALU.mult).then_inc(s_thr, 1)
                    dve.wait_ge(s_thr, 4)
                    dve.tensor_scalar(w_pos, w_flat, wsum[:, 2:3], None, ALU.is_gt).then_inc(s_tern, 1)
                elif s == 1:
                    dve.wait_ge(s_tern, 1)
                    dve.scalar_tensor_tensor(out=w_neg, in0=w_flat, scalar=wsum[:, 4:5], in1=w_pos,
                                             op0=ALU.is_lt, op1=ALU.subtract).then_inc(s_tern, 1)
                elif s == 2:
                    dve.wait_ge(s_tern, 2)
                    dve.scalar_tensor_tensor(out=w_pos, in0=w_neg, scalar=wsum[:, 3:4], in1=w_flat,
                                             op0=ALU.mult, op1=ALU.subtract).then_inc(s_tern, 1)
                elif s == 3:
                    dve.wait_ge(s_tern, 3)
                    dve.tensor_tensor(w_pos, w_pos, w_flat, ALU.add).then_inc(s_tern, 1)

            def low_linear(it):
                dve.wait_ge(s_wT_h, it + 1)
                dve.tensor_tensor(ffnT_l[:, it, :], pF[it % 2][:, :], ffnT_h[:, it, :].bitcast(F32),
                                  ALU.subtract).then_inc(s_wT_l, 1)

            def round_(c, first, more):
                for s in range(4 * QB):
                    if s < 4:
                        x_low(c, s)
                    if s == 4 and first:
                        dve.wait_ge(s_tables, 64)
                    if s in (5, 7, 9):
                        latent_row(c, (5, 7, 9).index(s))
                    if s in (4, 5, 7, 9):
                        rotary_key(c, (4, 5, 7, 9).index(s))
                    if first and s in LINEAR_SLOTS:
                        for it in LINEAR_SLOTS[s]:
                            low_linear(it)
                    if s in (8, 9, 10, 11):
                        linear(c, s - 8)
                    if s == 10:
                        latent_row(c, 3)
                    if more and s in (6, 7, 8, 9):
                        block_stats(c + 1, s - 6)
                    if more and s == 10:
                        moments_of_x(c + 1)
                    if s >= 12:
                        low_keys_transposed(c, s - 12)
                    weights(c, s // 4, s % 4)
                    if first:
                        quantise(s)
                    if more and s >= 12:
                        scale_x(c + 1, s - 12)

            rounds(ENG.DVE, round_)

        @block.tensor
        def _(pe):
            def transpose_x(c, b):
                n = QB * c + b
                pe.wait_ge(s_xhat, n + 1)
                if b >= 2:
                    pe.wait_ge(s_xT_l, n - 1)
                for it in range(IT):
                    mm = pe.transpose(pX[b % 2][:, it, :], xhat[:, b, it * P:(it + 1) * P], ident[:, :])
                mm.then_inc(s_xT, 1)

            def product(out, b, w_h, w_l, done):
                cols = slice(b * P, (b + 1) * P)
                for it in range(IT):
                    for k, (x, w) in enumerate(((0, w_h), (0, w_l), (1, w_h))):
                        mm = pe.matmul(out, xT[:, x, it, cols], w[:, it, :], start=(it == 0 and k == 0),
                                       stop=(it == IT - 1 and k == 2))
                mm.then_inc(done, 1)

            def latent(c, b):
                n = QB * c + b
                pe.wait_ge(s_xT_l, n + 1)
                need(pe, s_lat, n - 1)
                product(pKV[b % 2][:, 0:192], b, kvaT_h, kvaT_l, s_kv)

            def linear(c, b):
                if b >= 2:
                    pe.wait_ge(s_acc, QB * c + b - 1)
                elif b == 0:
                    need(pe, s_kT_l, QB * c)
                product(pF[b % 2][:, :], b, ffnT_h, ffnT_l, s_ffn)

            def transpose_keys(c, b):
                n = QB * c + b
                if b >= 2:
                    pe.wait_ge(s_kT_l, n - 1)
                else:
                    pe.wait_ge(s_acc, QB * (c + 1))
                keys = pF[1 - b % 2]
                pe.wait_ge(s_lat, n + 1)
                pe.transpose(keys[:, 0:P], lat[:, b, :], ident[:, :])
                pe.wait_ge(s_kpe_l, n + 1)
                pe.transpose(keys[:, P:2 * P], kpe[:, b, :, :].rearrange("p h f -> p (h f)").bitcast(F32),
                             ident[:, :]).then_inc(s_kT, 1)

            def weights(c, k, part):
                n, i = QB * c + k, k % 2
                if part == 0:
                    pe.wait_ge(s_load[i], 64 * (2 * c + k // 2 + 1))
                    need(pe, s_q_l, n)
                    for a in range(IT):
                        mm = pe.transpose(pW[0][:, a * P:(a + 1) * P], wo[i][:, a, :], ident[:, :])
                    mm.then_inc(s_woT, 1)
                elif part == 1:
                    half = slice(ROPE * i, ROPE * (i + 1))
                    pe.wait_ge(s_low, 3 * n + 2)
                    need(pe, s_v_l, n)
                    for x, w in enumerate((wqp_h, wqp_l)):
                        for it in range(IT):
                            mm = pe.matmul(pP[:, x, it, :], w[half, it * P:(it + 1) * P], order[half, :],
                                           start=True, stop=True)
                    mm.then_inc(s_pe, 1)
                elif part == 2:
                    pe.wait_ge(s_low, 3 * n + 3)
                    pe.wait_ge(s_woT_l, n + 1)
                    for it in range(IT):
                        cols = slice(it * P, (it + 1) * P)
                        for x, (a, b) in enumerate(((wqn_h, wkb_h), (wqn_h, wkb_l), (wqn_l, wkb_h))):
                            mm = pe.matmul(pQ[:, it, :], a[i][:, cols], b[i][:, 0, :], start=(x == 0), stop=(x == 2))
                    mm.then_inc(s_q, 1)
                else:
                    pe.wait_ge(s_pe_l, n + 1)
                    for x, (a, b) in enumerate(((wkb_h, woT_h), (wkb_h, woT_l), (wkb_l, woT_h))):
                        mm = pe.matmul(pW[1][:, :], a[i][:, 1, :], b[:, :], start=(x == 0), stop=(x == 2))
                    mm.then_inc(s_v, 1)

            pe.wait_ge(s_ones, 2)
            pe.wait_ge(s_const, 16 * 6)
            pe.matmul(pKV[0][:, :], ones[0:1, :], rows[:, 0:D], start=True, stop=True).then_inc(s_bcast, 1)
            pe.matmul(pKV[1][:, 0:RANK], ones[0:1, :], rows[:, D:], start=True, stop=True).then_inc(s_bcast, 1)
            for a in range(2):
                for it in range(IT):
                    mm = pe.transpose(pX[a][:, it, 0:96], w_kva[:, a, it * P:(it + 1) * P], ident[0:96, 0:96])
                mm.then_inc(s_aT, 1)
            pe.wait_ge(s_aT_l, 1)
            pe.wait_ge(s_bcast_out, 2)
            pe.wait_ge(s_order, 1)

            def transpose_linear(it):
                if it == 0:
                    pe.wait_ge(s_tern, 4)
                need(pe, s_wT_l, it - 1)
                for a in range(IT):
                    mm = pe.transpose(pF[it % 2][:, a * P:(a + 1) * P], w_ste[:, a, it * P:(it + 1) * P],
                                      ident[:, :])
                mm.then_inc(s_wT, 1)

            def round_(c, first, more):
                for s in range(4 * QB):
                    if s < 4:
                        transpose_x(c, s)
                    if s in (4, 5, 7, 9):
                        latent(c, (4, 5, 7, 9).index(s))
                    if first and s in LINEAR_SLOTS:
                        for it in LINEAR_SLOTS[s]:
                            transpose_linear(it)
                    if first and s == 8:
                        pe.wait_ge(s_wT_l, IT)
                    if s in (8, 9, 10, 11):
                        linear(c, s - 8)
                    if s >= 12:
                        transpose_keys(c, s - 12)
                    weights(c, s // 4, s % 4)
                    if first and s == 0:
                        pe.wait_ge(s_abs, 1)
                        pe.matmul(pF[1][:, 0:1], ones[:, :], wsum[:, 0:1], start=True, stop=True).then_inc(s_total, 1)

            rounds(ENG.PE, round_)


def build_attention(nc, t, keep, stored):
    with ExitStack() as ctx:
        def sb(name, shape, dt=F32):
            return ctx.enter_context(nc.sbuf_tensor(name, shape, dt))

        def ps(name, shape=(P, 512)):
            return ctx.enter_context(nc.psum_tensor(name, list(shape), F32))

        def sem(name):
            return ctx.enter_context(nc.semaphore(name))

        xT, Wq, Wp, Wv = (keep[k] for k in ("xT", "Wq", "Wp", "Wv"))
        cosT = [keep["cosT"], sb("cosT1", [P, CW])]
        sinT = [keep["sinT"], sb("sinT1", [P, CW])]
        acc = [keep["acc0"], sb("acc1", [P, QB, D])]
        q_h = [sb(f"q_h{i}", [P, CW], F32R) for i in range(2)]
        q_l = [sb(f"q_l{i}", [P, CW], F32R) for i in range(2)]
        qp_h = [sb(f"qp_h{i}", [P, CW], F32R) for i in range(2)]
        qp_l = [sb(f"qp_l{i}", [P, CW], F32R) for i in range(2)]
        probs = [sb(f"probs{i}", [P, QB, S]) for i in range(2)]
        pT_h = [sb(f"pT_h{i}", [P, CW], F32R) for i in range(PT_RING)]
        pT_l = [sb(f"pT_l{i}", [P, CW], F32R) for i in range(PT_RING)]
        o_h = sb("o_h", [P, CW], F32R)
        o_l = sb("o_l", [P, CW], F32R)
        rot_cos = sb("rot_cos", [P, CW])
        rot_sin = sb("rot_sin", [P, CW])
        rotated = sb("rotated", [P, CW])
        part_max = [sb(f"part_max{i}", [P, QB, NCH]) for i in range(2)]
        neg_max = [sb(f"neg_max{i}", [P, QB]) for i in range(2)]
        row_sum = [sb(f"row_sum{i}", [P, QB]) for i in range(2)]
        inv_sum = [sb(f"inv_sum{i}", [P, QB]) for i in range(2)]
        ident, ident16, mask = keep["ident"], keep["ident16"], keep["mask"]
        Kn_h, Kn_l, Kp = (keep[k] for k in ("Kn_h", "Kn_l", "Kp"))
        V_h, V_l = (keep[k][:, :].rearrange("p (n c) -> p n c", c=RANK) for k in ("V_h", "V_l"))

        p_score = [ps(f"p_score{i}") for i in range(2)]
        p_tr = [ps(f"p_tr{i}") for i in range(PT_RING)]
        p_out = ps("p_out")
        p_lat = ps("p_lat")
        p_rot = ps("p_rot")
        p_result = p_tr + [p_out]

        xT_in = sem("xT_in")
        tables_in = sem("tables_in")
        wq_in = [sem(f"wq_in{i}") for i in range(2)]
        wp_in = sem("wp_in")
        wv_in = [sem(f"wv_in{i}") for i in range(2)]
        result_out = sem("result_out")
        rot_projected = sem("rot_projected")
        lat_projected = sem("lat_projected")
        scored = sem("scored")
        transposed = sem("transposed")
        pv_done = sem("pv_done")
        out_projected = sem("out_projected")
        copied = sem("copied")
        maxed = sem("maxed")
        rot_read = sem("rot_read")
        pT_split = sem("pT_split")
        o_split = sem("o_split")
        q_split = sem("q_split")
        inverted = sem("inverted")
        accumulated = sem("accumulated")
        exped = sem("exped")
        pT_high = sem("pT_high")
        o_high = sem("o_high")
        q_high = sem("q_high")
        qp_high = sem("qp_high")
        rot_added = sem("rot_added")
        qp_ready = sem("qp_ready")

        block = ctx.enter_context(nc.Block())
        result = t["out"].rearrange("(c a p) o -> c p a o", a=QB, p=P)

        @block.sync
        def _(sp):
            def load_rotary(pos):
                sp.wait_ge(rot_projected, pairs_before(pos))
                sp.dma_start(Wp[:, :, :, :].bitcast(F32), t["wp_scr"][pos[1]]).then_inc(wp_in, 16)

            def load_q(pos):
                sp.wait_ge(lat_projected, heads_before(pos) - 1)
                sp.dma_start(Wq[pos[2]][:, :, :, :].bitcast(F32), t["wq_scr"][2 * pos[1] + pos[2]]).then_inc(wq_in[pos[2]], 16)

            def load_v(pos):
                sp.wait_ge(out_projected, QB * (heads_before(pos) - 1))
                sp.dma_start(Wv[pos[2]][:, :, :].bitcast(F32), t["wv_scr"][2 * pos[1] + pos[2]]).then_inc(wv_in[pos[2]], 16)

            def load_chunk(j):
                sp.wait_ge(lat_projected, H * j)
                sp.wait_ge(rot_projected, H // 2 * j)
                sp.dma_start(xT[:, :, :, :].bitcast(F32), t["xT_scr"][j]).then_inc(xT_in, 16)

            def load_tables(j):
                need(sp, rot_read, H // 2 * (j - 1))
                need(sp, result_out, 16 * (j - 1))
                sp.dma_start(cosT[j % 2][:, :], t["cosT"][j]).then_inc(tables_in, 16)
                sp.dma_start(sinT[j % 2][:, :], t["sinT"][j]).then_inc(tables_in, 16)
                sp.dma_start(acc[j % 2][:, :, :], t["acc_scr"][j]).then_inc(tables_in, 16)

            def store_chunk(j):
                sp.wait_ge(accumulated, QB * H * (j + 1))
                sp.dma_start(result[j], acc[j % 2][:, :, :]).then_inc(result_out, 16)

            for i in range(2):
                sp.wait_ge(stored["wq"][i], 16 * H // 2)
                sp.wait_ge(stored["wv"][i], 16 * H // 2)
            sp.wait_ge(stored["wp"], 16 * H // 2)
            sp.wait_ge(stored["xT"], 16 * (NCH - 1))
            sp.wait_ge(stored["acc"], 16 * (NCH - 1))
            for j in range(NCH):
                if j:
                    load_rotary((j, 0, 0))
                    load_q((j, 0, 0))
                    load_v((j - 1, H // 2 - 1, 0))
                    load_chunk(j)
                    load_q((j, 0, 1))
                    load_v((j - 1, H // 2 - 1, 1))
                load_rotary((j, 1, 0))
                for p in range(2):
                    load_q((j, 1, p))
                    if j:
                        load_v((j, 0, p))
                if j:
                    store_chunk(j - 1)
                if j + 1 < NCH:
                    load_tables(j + 1)
                with nc.Fori(2, H // 2, engines=[ENG.SP]) as m:
                    load_rotary((j, m, 0))
                    for p in range(2):
                        load_q((j, m, p))
                        load_v((j, m - 1, p))
            for p in range(2):
                load_v((NCH - 1, H // 2 - 1, p))
            store_chunk(NCH - 1)
            sp.wait_ge(result_out, 16 * NCH)

        @block.tensor
        def _(pe):
            def project_rotary(pos):
                need(pe, wp_in, 16 * pairs_before(pos))
                if first_of_chunk(pos):
                    need(pe, xT_in, 16 * pos[0])
                need(pe, rot_read, pairs_before(pos))
                for it in range(IT):
                    mm = product(p_rot[:, :], Wp, it)
                mm.then_inc(rot_projected, 1)

            def project_latent(pos, it):
                g, p = heads_before(pos), pos[2]
                if it == 0:
                    need(pe, wq_in[p], 16 * pairs_before(pos))
                    need(pe, q_split, g)
                mm = product(p_lat[:, :], Wq[p], it)
                if it == IT - 1:
                    mm.then_inc(lat_projected, 1)

            def product(out, weights, it):
                for k, (w, x) in enumerate(((0, 0), (0, 1), (1, 0))):
                    mm = pe.matmul(out, weights[:, w, it, :], xT[:, x, it, :], start=(it == 0 and k == 0),
                                   stop=(it == IT - 1 and k == 2))
                return mm

            def scores(pos, u):
                j, p = pos[0], pos[2]
                i, b = u // (j + 1), u % (j + 1)
                width = P * (i + 1) if b == j else CW
                if u == 0:
                    pe.wait_ge(q_split, heads_before(pos) + 1)
                need(pe, copied, tiles_before(pos) + u - 1)
                rows, keys = slice(i * P, (i + 1) * P), slice(b * CW, b * CW + width)
                out = p_score[u % 2]
                for k, (q, kk) in enumerate(((q_h, Kn_h), (q_h, Kn_l), (q_l, Kn_h), (qp_h, Kp), (qp_l, Kp))):
                    if u == 0 and k == 3:
                        pe.wait_ge(qp_ready, 2 * heads_before(pos) + 2)
                    mm = pe.matmul(out[:, 0:width], q[p][:, rows], kk[:, keys], start=(k == 0),
                                   stop=(k == 4 and b < j))
                if b == j:
                    mm = pe.matmul(out[:, width - P:width], ident16[:, :], mask[:, :], start=False, stop=True)
                mm.then_inc(scored, 1)

            def transposes(pos, k):
                n, p = tiles_before(pos), pos[2]
                if k == 0:
                    pe.wait_ge(exped, rows_before(pos) + QB)
                if k >= PT_RING:
                    need(pe, pT_split, n + k - PT_RING + 1)
                else:
                    need(pe, accumulated, QB * (heads_before(pos) - 1) + k + 1)
                for i in range(first_row(pos, k), QB):
                    mm = pe.transpose(p_tr[k % PT_RING][:, i * P:(i + 1) * P], probs[p][:, i, k * P:(k + 1) * P],
                                      ident[:, :])
                mm.then_inc(transposed, 1)

            def values(pos, k):
                if k == 0:
                    need(pe, accumulated, QB * heads_before(pos))
                pe.wait_ge(pT_split, tiles_before(pos) + k + 1)
                cols, r = slice(first_row(pos, k) * P, CW), k % PT_RING
                last = k == tiles_of(pos) - 1
                for a, (v, pt) in enumerate(((V_h, pT_h), (V_h, pT_l), (V_l, pT_h))):
                    mm = pe.matmul(p_out[:, cols], v[:, k, :], pt[r][:, cols], start=(k == 0 and a == 0),
                                   stop=(last and a == 2))
                mm.then_inc(pv_done, 1)

            def project_out(pos, i):
                g, p = heads_before(pos), pos[2]
                if i == 0:
                    pe.wait_ge(o_split, g + 1)
                    need(pe, wv_in[p], 16 * pairs_before(pos))
                out, rows = p_result[i], slice(i * P, (i + 1) * P)
                for k, (o, w) in enumerate(((o_h, 0), (o_h, 1), (o_l, 0))):
                    mm = pe.matmul(out[:, :], o[:, rows], Wv[p][:, w, :], start=(k == 0), stop=(k == 2))
                mm.then_inc(out_projected, 1)

            def step(cur, prev, nxt):
                units = tiles_of(cur) if cur else tiles_of(prev)
                tiles = tiles_of(prev) if prev else 0
                done = 0
                for u in range(units):
                    if cur:
                        scores(cur, u)
                    if u < tiles:
                        transposes(prev, u)
                    if u >= 2 and u - 2 < tiles:
                        values(prev, u - 2)
                        done = u - 1
                    if nxt and u == rotary_unit(nxt, units):
                        project_rotary(nxt)
                order = ["q", "v", "q", "v", "q", "q"] if units == QB else ["q", "v", "v", "q", "q", "q"]
                it = 0
                for what in order:
                    if what == "v" and done < tiles:
                        values(prev, done)
                        done += 1
                    if what == "q" and nxt:
                        project_latent(nxt, it)
                        it += 1
                if prev:
                    for i in range(QB):
                        project_out(prev, i)

            project_rotary((0, 0, 0))
            for it in range(IT):
                project_latent((0, 0, 0), it)
            walk(nc, ENG.PE, step)

        @block.vector
        def _(dve):
            def copy_scores(pos, u):
                j, p = pos[0], pos[2]
                i, b = u // (j + 1), u % (j + 1)
                width = P * (i + 1) if b == j else CW
                n = tiles_before(pos) + u
                dve.wait_ge(scored, n + 1)
                dve.tensor_scalar(probs[p][:, i, b * CW:b * CW + width], p_score[u % 2][:, 0:width], SCALE, LOWEST,
                                  ALU.mult, ALU.max, accum_out=part_max[p][:, i, b:b + 1]).then_inc(copied, 1)
                if b == j:
                    dve.wait_ge(copied, n + 1)
                    need(dve, exped, rows_before(pos) - QB)
                    dve.tensor_reduce(neg_max[p][:, i:i + 1], part_max[p][:, i, 0:j + 1], AXX, ALU.max,
                                      negate=True).then_inc(maxed, 1)

            def split_tile(pos, k):
                r, cols = k % PT_RING, slice(first_row(pos, k) * P, CW)
                dve.wait_ge(pT_high, tiles_before(pos) + k + 1)
                dve.tensor_tensor(pT_l[r][:, cols], p_tr[r][:, cols], pT_h[r][:, cols].bitcast(F32),
                                  ALU.subtract).then_inc(pT_split, 1)

            def rotate(pos, op):
                if op == 0:
                    if first_of_chunk(pos):
                        need(dve, tables_in, 48 * pos[0])
                    dve.wait_ge(rot_projected, pairs_before(pos) + 1)
                    need(dve, rot_added, pairs_before(pos))
                    dve.tensor_tensor(rot_cos[:, :], p_rot[:, :], cosT[pos[0] % 2][:, :], ALU.mult)
                else:
                    q = op - 1
                    to, of = slice(HALF * q, HALF * (q + 1)), slice(HALF * (q ^ 1), HALF * ((q ^ 1) + 1))
                    last = dve.tensor_tensor(rot_sin[to, :], p_rot[of, :], sinT[pos[0] % 2][of, :], ALU.mult)
                    if op == 4:
                        last.then_inc(rot_read, 1)

            def split_query(pos):
                p = pos[2]
                dve.wait_ge(q_high, heads_before(pos) + 1)
                dve.tensor_tensor(q_l[p][:, :], p_lat[:, :], q_h[p][:, :].bitcast(F32), ALU.subtract).then_inc(q_split, 1)

            def split_output(pos):
                dve.wait_ge(o_high, heads_before(pos) + 1)
                dve.tensor_tensor(o_l[:, :], p_out[:, :], o_h[:, :].bitcast(F32), ALU.subtract).then_inc(o_split, 1)

            def accumulate(pos):
                g, p = heads_before(pos), pos[2]
                a = acc[pos[0] % 2]
                dve.wait_ge(exped, rows_before(pos) + QB)
                need(dve, accumulated, QB * g)
                dve.reciprocal(inv_sum[p][:, :], row_sum[p][:, :]).then_inc(inverted, 1)
                dve.wait_ge(inverted, g + 1)
                for i in range(QB):
                    dve.wait_ge(out_projected, QB * g + i + 1)
                    dve.scalar_tensor_tensor(out=a[:, i, :], in0=p_result[i][:, :],
                                             scalar=inv_sum[p][:, i:i + 1], in1=a[:, i, :],
                                             op0=ALU.mult, op1=ALU.add).then_inc(accumulated, 1)

            def step(cur, prev, nxt):
                units = tiles_of(cur) if cur else tiles_of(prev)
                tiles = tiles_of(prev) if prev else 0
                for u in range(units):
                    if cur:
                        copy_scores(cur, u)
                    if u < tiles:
                        split_tile(prev, u)
                    for op in range(5):
                        if nxt and nxt[2] == 0 and u == min(rotary_unit(nxt, units) + op // 3, units - 1):
                            rotate(nxt, op)
                if prev:
                    split_output(prev)
                if nxt:
                    split_query(nxt)
                if prev:
                    accumulate(prev)

            for op in range(5):
                rotate((0, 0, 0), op)
            split_query((0, 0, 0))
            walk(nc, ENG.DVE, step)

        @block.scalar
        def _(act):
            def exp_row(pos, i):
                p, width = pos[2], P * (QB * pos[0] + i + 1)
                act.wait_ge(maxed, rows_before(pos) + i + 1)
                need(act, inverted, heads_before(pos) - 1)
                act.activation(probs[p][:, i, 0:width], probs[p][:, i, 0:width], ACT.Exp,
                               bias=neg_max[p][:, i:i + 1], scale=1.0,
                               accum_out=row_sum[p][:, i:i + 1]).then_inc(exped, 1)

            def high_tile(pos, k):
                r, cols, n = k % PT_RING, slice(first_row(pos, k) * P, CW), tiles_before(pos)
                act.wait_ge(transposed, n + k + 1)
                need(act, pv_done, n + k - PT_RING + 1 if k >= PT_RING else n)
                act.activation(pT_h[r][:, cols], p_tr[r][:, cols], ACT.Copy).then_inc(pT_high, 1)

            def high_output(pos):
                g = heads_before(pos)
                act.wait_ge(pv_done, tiles_before(pos) + tiles_of(pos))
                need(act, out_projected, QB * g)
                act.activation(o_h[:, :], p_out[:, :], ACT.Copy).then_inc(o_high, 1)

            def high_query(pos):
                act.wait_ge(lat_projected, heads_before(pos) + 1)
                free_query(pos)
                act.activation(q_h[pos[2]][:, :], p_lat[:, :], ACT.Copy).then_inc(q_high, 1)

            def high_rotary(pos):
                p = pos[2]
                act.wait_ge(rot_added, pairs_before(pos) + 1)
                free_query(pos)
                for half in (slice(0, ROPE), slice(ROPE, P)):
                    last = act.activation(qp_h[p][half, :], rotated[ROPE * p:ROPE * (p + 1), :], ACT.Copy)
                last.then_inc(qp_high, 1)

            def free_query(pos):
                j, m, p = pos
                if first_of_chunk(pos):
                    need(act, scored, tiles_before((j - 1, H // 2 - 1, 1)) if j else 0)
                else:
                    need(act, scored, tiles_before((j, m, 0)) if p else tiles_before((j, m - 1, 1)))

            def step(cur, prev, nxt):
                units = tiles_of(cur) if cur else tiles_of(prev)
                tiles = tiles_of(prev) if prev else 0
                for u in range(units):
                    if u < tiles:
                        high_tile(prev, u)
                    if cur and (u + 1) % (cur[0] + 1) == 0 and u + 1 < units:
                        exp_row(cur, u // (cur[0] + 1))
                    if cur and cur[2] == 0 and u == 1:
                        high_rotary(nxt)
                early = cur and nxt and cur[0] > 0 and not first_of_chunk(nxt)
                if nxt and nxt[2] == 0 and early:
                    high_rotary(nxt)
                if prev:
                    high_output(prev)
                if cur:
                    exp_row(cur, QB - 1)
                if nxt and nxt[2] == 0 and not early:
                    high_rotary(nxt)
                if nxt:
                    high_query(nxt)

            high_query((0, 0, 0))
            high_rotary((0, 0, 0))
            walk(nc, ENG.Activation, step)

        @block.gpsimd
        def _(pool):
            def add_rotary(pos):
                pool.wait_ge(rot_read, pairs_before(pos) + 1)
                need(pool, qp_ready, 2 * heads_before(pos))
                pool.tensor_tensor(rotated[:, :], rot_cos[:, :], rot_sin[:, :], ALU.add).then_inc(rot_added, 1)

            def low_rotary(pos):
                p = pos[2]
                own = slice(ROPE * p, ROPE * (p + 1))
                pool.wait_ge(qp_high, heads_before(pos) + 1)
                if p:
                    pool.wait_ge(qp_ready, 2 * heads_before(pos))
                else:
                    pool.wait_ge(rot_added, pairs_before(pos) + 1)
                pool.tensor_tensor(qp_l[p][0:ROPE, :], rotated[own, :], qp_h[p][own, :].bitcast(F32),
                                   ALU.subtract).then_inc(qp_ready, 1)
                pool.wait_ge(qp_ready, 2 * heads_before(pos) + 1)
                pool.tensor_tensor(qp_l[p][ROPE:P, :], rotated[own, :], qp_h[p][own, :].bitcast(F32),
                                   ALU.subtract).then_inc(qp_ready, 1)

            def step(cur, prev, nxt):
                if nxt and nxt[2] == 0:
                    add_rotary(nxt)
                if nxt:
                    low_rotary(nxt)

            add_rotary((0, 0, 0))
            low_rotary((0, 0, 0))
            walk(nc, ENG.Pool, step)


def build(nc, t):
    with ExitStack() as ctx:
        def sb(name, shape, dt=F32):
            return ctx.enter_context(nc.sbuf_tensor(name, shape, dt))

        keep = {
            "ident": sb("ident", [P, P]),
            "ident16": sb("ident16", [P, P], BF16),
            "mask": sb("mask_bf16", [P, P], BF16),
            "mask_f32": sb("mask_f32", [P, P]),
            "order_f32": sb("order_f32", [P, ROPE]),
            "Kn_h": sb("Kn_h", [P, S], F32R),
            "Kn_l": sb("Kn_l", [P, S], F32R),
            "Kp": sb("Kp", [P, S], F32R),
            "V_h": sb("V_h", [P, NT * RANK], F32R),
            "V_l": sb("V_l", [P, NT * RANK], F32R),
            "xT": sb("xT", [P, 2, IT, CW], F32R),
            "acc0": sb("acc0", [P, QB, D]),
            "cosT": sb("cosT_sb", [P, CW]),
            "sinT": sb("sinT_sb", [P, CW]),
            "Wq": [sb(f"Wq{i}", [P, 2, IT, P], F32R) for i in range(2)],
            "Wp": sb("Wp", [P, 2, IT, P], F32R),
            "Wv": [sb(f"Wv{i}", [P, 2, D], F32R) for i in range(2)],
        }
        stored = {k: ctx.enter_context(nc.semaphore(f"{k}_stored")) for k in ("xT", "acc", "wp")}
        for k in ("wq", "wv"):
            stored[k] = [ctx.enter_context(nc.semaphore(f"{k}_stored{i}")) for i in range(2)]
        build_prepare(nc, t, keep, stored)
        build_attention(nc, t, keep, stored)


def constants():
    freqs = 1.0 / 10000.0 ** (np.arange(0, ROPE, 2, dtype=np.float32) / ROPE)
    ang = np.outer(np.arange(S, dtype=np.float32), freqs)
    cos, sin = np.cos(ang), np.sin(ang)
    by_token = lambda a: np.ascontiguousarray(np.concatenate([a, a], 1).reshape(NT, P, ROPE).transpose(1, 0, 2))
    by_chunk = lambda a: np.ascontiguousarray(a.T.reshape(P, NCH, CW).transpose(1, 0, 2))
    order = np.zeros((2, ROPE, ROPE), np.float32)
    for x in range(2):
        for f in range(HALF):
            order[:, 2 * f + x, HALF * x + f] = 1.0
    return {
        "ident": np.eye(P, dtype=np.float32),
        "mask": np.where(np.tril(np.ones((P, P), bool)), 0.0, MASKED).astype(np.float32),
        "order": order.reshape(P, ROPE),
        "cosN": by_token(cos),
        "sinN": by_token(sin),
        "cosT": by_chunk(np.concatenate([cos] * 4, 1)),
        "sinT": by_chunk(np.concatenate([sin, -sin, sin, -sin], 1)),
    }


_INS = {"x": "L0_attn_x", "wq": "L0_attn_wq", "wkv_a": "L0_attn_wkv_a", "wkv_b": "L0_attn_wkv_b",
        "wo": "L0_attn_wo", "kv_norm_w": "L0_attn_kv_norm_w", "w_ffn": "L0_ffn_weight", "b_ffn": "L0_ffn_bias"}


def kernel(**inputs):
    import concourse.bacc as bacc
    from concourse.bass_utils import run_bass_kernel_spmd

    arrays = {name: np.ascontiguousarray(inputs[key]) for name, key in _INS.items()}
    arrays["x"] = arrays["x"].reshape(S, D)
    arrays.update(constants())
    nc = bacc.Bacc("TRN2", target_bir_lowering=False, num_devices=1)
    t, feeds = {}, {}
    for name, a in arrays.items():
        t[name] = nc.dram_tensor(f"in_{name}", a.shape, F32, kind="ExternalInput").ap()
        feeds[f"in_{name}"] = a
    t["out"] = nc.dram_tensor("out_0", (S, D), F32, kind="ExternalOutput").ap()
    for name, shape, dt in (("xT_scr", (NCH, P, 2, IT, CW), F32), ("acc_scr", (NCH, P, QB, D), F32),
                            ("wq_scr", (H, P, 2, IT, P), F32), ("wp_scr", (H // 2, P, 2, IT, P), F32),
                            ("wv_scr", (H, P, 2, D), F32)):
        t[name] = nc.dram_tensor(name, shape, dt, kind="Internal").ap()
    build(nc, t)
    r = run_bass_kernel_spmd(nc, [feeds], core_ids=[0])
    return r.results[0]["out_0"].reshape(1, S, D)
```
